# Optimizing a Trainium2 kernel written in Bass

```python
import numpy as np
import jax
import jax.numpy as jnp

def _softmax(x, axis=-1):
    return jax.nn.softmax(x, axis=axis)

def _gelu(x):
    return jax.nn.gelu(x, approximate=True)

def _silu(x):
    return jax.nn.silu(x)

def _sigmoid(x):
    return jax.nn.sigmoid(x)

def _layernorm(x, axis=-1, eps=1e-05):
    m = jnp.mean(x, axis=axis, keepdims=True)
    v = jnp.var(x, axis=axis, keepdims=True)
    return (x - m) / jnp.sqrt(v + eps)

def _scatter_add(tgt, idx, src, axis=0):
    return tgt.at[idx].add(src)

def _segment_sum(src, seg, n):
    return jax.ops.segment_sum(src, seg, n)
kernel_name = 'mk_xattn_ffn_d1_seqx_r4_625a29'

def setup_inputs(seed: int=0):
    np.random.seed(seed)
    _w = jnp.asarray

    def _rec_inputs():
        import jax
        import jax.numpy as jnp
        _rk = jax.random.key(seed)
        x = -0.0002928 + 1 * jax.random.normal(jax.random.fold_in(_rk, 1), (4, 1024, 256), jnp.float32)
        _lenS = 1024 - jax.random.randint(jax.random.fold_in(_rk, 7), (4,), 0, max(1, 1024 // 4) + 1, jnp.int32)
        _lenS2 = 154 - jax.random.randint(jax.random.fold_in(_rk, 8), (4,), 0, max(1, 154 // 4) + 1, jnp.int32)
        _ctx_1024P = jax.random.normal(jax.random.fold_in(_rk, 11), (4, 16, 256), jnp.float32)
        _ctx_1024c = jax.random.dirichlet(jax.random.fold_in(_rk, 511), 0.3 * jnp.ones((16,), jnp.float32), (4, 154))
        _ctx_1024t = jnp.einsum('bsk,bkd->bsd', _ctx_1024c, _ctx_1024P)
        _ctx_1024t = _ctx_1024t * jax.lax.rsqrt(jnp.mean(jnp.square(_ctx_1024t)) + 1e-12) * 0.953939
        ctx_1024 = -1.39393e-06 + 0.999914 * (_ctx_1024t + 0.3 * jax.random.normal(jax.random.fold_in(_rk, 611), (4, 154, 256), jnp.float32))
        return (x, ctx_1024)
    x, ctx_1024 = _rec_inputs()

    def _L0_xattn_setup():
        import jax, jax.numpy as jnp
        import numpy as np
        NUM_HEADS = 16
        D_MODEL = 256
        HEAD_DIM = D_MODEL // NUM_HEADS
        SCALE = 8.0 / HEAD_DIM
        LN_EPS = 1e-05

        def _layernorm(x, g, b):
            mu = jnp.mean(x, axis=-1, keepdims=True)
            var = jnp.mean(jnp.square(x - mu), axis=-1, keepdims=True)
            return (x - mu) * jax.lax.rsqrt(var + LN_EPS) * g + b
        key = jax.random.key(seed)
        ks = jax.random.split(key, 8)
        B, N, M = (2, 512, 512)
        std = 1.0 / np.sqrt(D_MODEL)
        return {'x1': jax.random.normal(ks[0], (B, N, D_MODEL), jnp.float32), 'x2': jax.random.normal(ks[1], (B, M, D_MODEL), jnp.float32), 'Wq': jax.random.normal(ks[2], (D_MODEL, D_MODEL), jnp.float32) * std, 'Wk': jax.random.normal(ks[3], (D_MODEL, D_MODEL), jnp.float32) * std, 'Wv': jax.random.normal(ks[4], (D_MODEL, D_MODEL), jnp.float32) * std, 'Wp': jax.random.normal(ks[5], (D_MODEL, D_MODEL), jnp.float32) * std, 'bp': jnp.zeros((D_MODEL,), jnp.float32), 'ln_g': jnp.ones((HEAD_DIM,), jnp.float32), 'ln_b': jnp.zeros((HEAD_DIM,), jnp.float32)}
    _L0_xattn_all = _L0_xattn_setup()
    _L0_xattn_in = {k: v for k, v in _L0_xattn_all.items() if k in ('Wq', 'Wk', 'Wv', 'Wp', 'bp', 'ln_g', 'ln_b')}
    del _L0_xattn_all

    def _L0_ffn_setup():
        import jax, jax.numpy as jnp
        import numpy as np
        DIM = 256

        def _reference_tuple_inner(x, W_r, W_k, W_v, mu_r, mu_k):
            B, T, C = x.shape
            x_prev = jnp.concatenate([jnp.zeros((B, 1, C), x.dtype), x[:, :-1, :]], axis=1)
            xr = mu_r * x + (1.0 - mu_r) * x_prev
            xk = mu_k * x + (1.0 - mu_k) * x_prev
            r = jax.nn.sigmoid(jnp.einsum('btc,dc->btd', xr, W_r))
            k = jnp.einsum('btc,dc->btd', xk, W_k)
            k_act = jnp.square(jax.nn.relu(k))
            out = r * jnp.einsum('btc,dc->btd', k_act, W_v)
            new_state = x[:, -1, :]
            return (out, new_state)
        key = jax.random.key(seed)
        ks = jax.random.split(key, 6)
        B, T, C = (8, 512, DIM)
        x = jax.random.normal(ks[0], (B, T, C), dtype=jnp.float32)
        s = 1.0 / np.sqrt(C)
        W_r = jax.random.uniform(ks[1], (C, C), jnp.float32, -s, s)
        W_k = jax.random.uniform(ks[2], (C, C), jnp.float32, -s, s)
        W_v = jax.random.uniform(ks[3], (C, C), jnp.float32, -s, s)
        mu_r = jax.random.uniform(ks[4], (C,), jnp.float32)
        mu_k = jax.random.uniform(ks[5], (C,), jnp.float32)
        return {'x': x, 'W_r': W_r, 'W_k': W_k, 'W_v': W_v, 'mu_r': mu_r, 'mu_k': mu_k}
    _L0_ffn_all = _L0_ffn_setup()
    _L0_ffn_in = {k: v for k, v in _L0_ffn_all.items() if k in ('W_r', 'W_k', 'W_v', 'mu_r', 'mu_k')}
    del _L0_ffn_all
    return {'x': x, 'ctx_1024': ctx_1024, 'L0_xattn_Wq': _L0_xattn_in['Wq'], 'L0_xattn_Wk': _L0_xattn_in['Wk'], 'L0_xattn_Wv': _L0_xattn_in['Wv'], 'L0_xattn_Wp': _L0_xattn_in['Wp'], 'L0_xattn_bp': _L0_xattn_in['bp'], 'L0_xattn_ln_g': _L0_xattn_in['ln_g'], 'L0_xattn_ln_b': _L0_xattn_in['ln_b'], 'L0_ffn_W_r': _L0_ffn_in['W_r'], 'L0_ffn_W_k': _L0_ffn_in['W_k'], 'L0_ffn_W_v': _L0_ffn_in['W_v'], 'L0_ffn_mu_r': _L0_ffn_in['mu_r'], 'L0_ffn_mu_k': _L0_ffn_in['mu_k']}

def reference(x, ctx_1024, L0_xattn_Wq, L0_xattn_Wk, L0_xattn_Wv, L0_xattn_Wp, L0_xattn_bp, L0_xattn_ln_g, L0_xattn_ln_b, L0_ffn_W_r, L0_ffn_W_k, L0_ffn_W_v, L0_ffn_mu_r, L0_ffn_mu_k):
    import jax
    import jax.numpy as jnp

    def _L0_xattn_ref(x1, x2, Wq, Wk, Wv, Wp, bp, ln_g, ln_b):
        import jax, jax.numpy as jnp
        import numpy as np
        NUM_HEADS = 16
        D_MODEL = 256
        HEAD_DIM = D_MODEL // NUM_HEADS
        SCALE = 8.0 / HEAD_DIM
        LN_EPS = 1e-05

        def _layernorm(x, g, b):
            mu = jnp.mean(x, axis=-1, keepdims=True)
            var = jnp.mean(jnp.square(x - mu), axis=-1, keepdims=True)
            return (x - mu) * jax.lax.rsqrt(var + LN_EPS) * g + b
        B, N, C = x1.shape
        M = x2.shape[1]
        H, D = (NUM_HEADS, HEAD_DIM)
        q = (x1 @ Wq.T).reshape(B, N, H, D).transpose(0, 2, 1, 3)
        k = (x2 @ Wk.T).reshape(B, M, H, D).transpose(0, 2, 1, 3)
        v = (x2 @ Wv.T).reshape(B, M, H, D).transpose(0, 2, 1, 3)
        q = _layernorm(q, ln_g, ln_b)
        k = _layernorm(k, ln_g, ln_b)
        q = q * SCALE
        attn = jnp.einsum('bhnd,bhmd->bhnm', q, k)
        attn = jax.nn.softmax(attn, axis=-1)
        out = jnp.einsum('bhnm,bhmd->bhnd', attn, v)
        out = out.transpose(0, 2, 1, 3).reshape(B, N, C)
        return out @ Wp.T + bp

    def _L0_ffn_ref(x, W_r, W_k, W_v, mu_r, mu_k):
        import jax, jax.numpy as jnp
        import numpy as np
        DIM = 256

        def _reference_tuple_inner(x, W_r, W_k, W_v, mu_r, mu_k):
            B, T, C = x.shape
            x_prev = jnp.concatenate([jnp.zeros((B, 1, C), x.dtype), x[:, :-1, :]], axis=1)
            xr = mu_r * x + (1.0 - mu_r) * x_prev
            xk = mu_k * x + (1.0 - mu_k) * x_prev
            r = jax.nn.sigmoid(jnp.einsum('btc,dc->btd', xr, W_r))
            k = jnp.einsum('btc,dc->btd', xk, W_k)
            k_act = jnp.square(jax.nn.relu(k))
            out = r * jnp.einsum('btc,dc->btd', k_act, W_v)
            new_state = x[:, -1, :]
            return (out, new_state)
        return _reference_tuple_inner(x, W_r, W_k, W_v, mu_r, mu_k)[0]
    x = x + _L0_xattn_ref(_layernorm(x, axis=-1), ctx_1024, L0_xattn_Wq, L0_xattn_Wk, L0_xattn_Wv, L0_xattn_Wp, L0_xattn_bp, L0_xattn_ln_g, L0_xattn_ln_b)
    x = x + _L0_ffn_ref(_layernorm(x, axis=-1), L0_ffn_W_r, L0_ffn_W_k, L0_ffn_W_v, L0_ffn_mu_r, L0_ffn_mu_k)
    return x

_drawn_inputs = setup_inputs


def setup_inputs(seed=0):
    import zlib

    import numpy as np

    out = dict(_drawn_inputs(seed))
    spreads = {'L0_xattn_bp': (0.0, 0.1), 'L0_xattn_ln_g': (1.0, 0.2), 'L0_xattn_ln_b': (0.0, 0.324)}
    factors = {'L0_ffn_W_r': 3.42, 'L0_ffn_mu_r': 7.941}
    for name, (base, spread) in spreads.items():
        noise = np.random.default_rng([zlib.crc32(name.encode()), seed]).standard_normal(out[name].shape)
        drawn = base * np.exp(spread * noise) if base else spread * noise
        out[name] = jnp.asarray(drawn.astype(out[name].dtype))
    for name, factor in factors.items():
        out[name] = (out[name] * factor).astype(out[name].dtype)
    return out
```

```python
from contextlib import ExitStack

import numpy as np

import concourse.bass as bass
from concourse import mybir

ALU = mybir.AluOpType
ACT = mybir.ActivationFunctionType
F32 = mybir.dt.float32
F32R = mybir.dt.float32r
I32 = mybir.dt.int32
AX_X = mybir.AxisListType.X

P = 128
B, N, C = 4, 1024, 256
M, H, D = 154, 16, 16
SCALE = 8.0 / D
EPS = 1e-5
T = 512
BLOCKS = B * N // T
J = T // P
KC = C // P
G = H // 2
GROUPS = H // 4
M0, M1 = P, M - P
SLOT = 32
KPAD = M + 6

ROW_HI, ROW_HI2, ROW_LO, ROW_ONE, ROW_MAX, ROWS = 0, 32, 64, 96, 98, 102
WK, WV, WQ, WP, FR, FK, FV = range(7)
NW = 7
AUX_MU_R, AUX_MU_K, AUX_G, AUX_B, AUX_BP, AUX_ID = 0, 2, 4, 20, 36, 36 + C
AUX = AUX_ID + P


def wait(eng, sem, value):
    if isinstance(value, int) and value <= 0:
        return
    eng.wait_ge(sem, value)


class Steps:

    def __init__(self, eng, sem, before):
        self.eng, self.sem, self.before, self.n = eng, sem, before, 0

    def then(self, ins):
        self.n += 1
        ins.then_inc(self.sem, 1)
        self.eng.wait_ge(self.sem, self.before + self.n)


def xattn_ffn(nc, x, context, weights, aux, out):
    x_rows = x.rearrange("(t j p) c -> t p j c", j=J, p=P)
    out_rows = out.rearrange("(t j p) c -> t p j c", j=J, p=P)

    with ExitStack() as stack:
        def sb(name, shape, dt=F32):
            return stack.enter_context(nc.sbuf_tensor(name, shape, dt))

        def ps(name, shape):
            return stack.enter_context(nc.psum_tensor(name, shape, F32))

        def sem(name):
            return stack.enter_context(nc.semaphore(name))

        w = sb("w", [P, KC, NW, C])
        aux_sb = sb("aux_sb", [P, AUX])
        ident = aux_sb[:, AUX_ID:AUX_ID + P]
        minus_half = sb("minus_half", [P, J])
        eps = sb("eps", [P, J])
        spare = sb("spare", [P, 2])
        gs = sb("gs", [P, 2, D])
        wsum = sb("wsum", [P, 2, KC, H])
        cx = sb("cx", [P, KC, 2 * P])
        kb = sb("kb", [P, 2, G, 2, KPAD], F32R)
        kr = sb("kr", [P, 2, G, P], F32R)
        vm = sb("vm", [P, 2, H, SLOT])
        vr = sb("vr", [P, 2, GROUPS, P])
        ks = sb("ks", [P, 2, G, 2, ROWS])
        kf = sb("kf", [P, 2, C])
        kt = sb("kt", [P, 2, C])
        kst = sb("kst", [P, 5, 2 * H])
        x_in = sb("x_in", [P, 2, J, C])
        st = sb("st", [P, 2, J, 6])
        mv = sb("mv", [P, 2, J, 2])
        ve = sb("ve", [P, 2, J])
        rs = sb("rs", [P, 2, J])
        xn = sb("xn", [P, J, C])
        x1t = sb("x1t", [P, KC, T])
        qn = sb("qn", [P, J, C])
        qst = sb("qst", [P, 5, J * H])
        qh = sb("qh", [P, KC, T])
        ql = sb("ql", [P, KC, T])
        xq = sb("xq", [P, 2, G, T], F32R)
        nmax = sb("nmax", [P, J, H])
        cs = sb("cs", [P, J, G, 4])
        ct = sb("ct", [4 * G, T])
        e = sb("e", [P, 10, T])
        osb = sb("osb", [P, 2, T])
        rl = sb("rl", [P, J, 4])
        on = sb("on", [P, J, C])
        ot = sb("ot", [P, KC, T])
        xb = sb("xb", [P, 2, J, C])
        x2 = sb("x2", [P, J, C])
        x2t = sb("x2t", [P, 2, KC, T + 1])
        xd = sb("xd", [P, KC, T])
        xr = sb("xr", [P, KC, T])
        xk = sb("xk", [P, KC, T])
        rt = sb("rt", [P, J, C])

        ps_a = ps("ps_a", [P, 3, T])
        ps_b = ps("ps_b", [P, 2, T])
        ps_o = ps("ps_o", [P, T])
        ps_w = ps("ps_w", [P, 2, T])

        def sems(text):
            return [sem(name) for name in text.split()]

        aux_in, w_in, w_rest_in, cx_in, zeroed, centred, w_steps = sems("aux_in w_in w_rest_in cx_in zeroed centred w_steps")
        x_in_landed, stacked, max_placed = (sems(f"{n}0 {n}1") for n in ("x_landed", "stacked", "max_placed"))
        k_steps, ks_ready, keys_odd = sems("k_steps ks_ready keys_odd")
        mv1_ready, rs1_ready, xn1_ready, x1t_ready, x1t_copied = sems("mv1_ready rs1_ready xn1_ready x1t_ready x1t_copied")
        q_ready, q_squared, q_steps, qn_ready = sems("q_ready q_squared q_steps qn_ready")
        qt_ready, qh_ready, ql_ready = sems("qt_ready qh_ready ql_ready")
        b_ready, b_read = sems("b_ready b_read")
        c_steps, cs_ready, ct_ready, ct_copied = sems("c_steps cs_ready ct_ready ct_copied")
        a_ready, e_ready, o_ready, o_copied, on_t_ready, o_steps, on_ready = sems(
            "a_ready e_ready o_ready o_copied on_t_ready o_steps on_ready")
        ot_ready, ot_copied, y_ready, xb_ready, x2_ready = sems("ot_ready ot_copied y_ready xb_ready x2_ready")
        mv2_ready, rs2_ready, xn2_ready, x2t_ready, x2t_copied = sems("mv2_ready rs2_ready xn2_ready x2t_ready x2t_copied")
        ln1_steps, ln2_steps, p_steps, xd_ready, xr_ready, xk_ready = sems(
            "ln1_steps ln2_steps p_steps xd_ready xr_ready xk_ready")
        ln_steps = (ln1_steps, ln2_steps)
        k2_ready, relu_ready, kact_ready = sems("k2_ready relu_ready kact_ready")
        r_ready, gate_ready, kv2_ready, gated, out_ready, stored, carried = sems(
            "r_ready gate_ready kv2_ready gated out_ready stored carried")

        ZEROED = 13
        KEY_BANKS, MAX_BANKS = 8, J * G

        def banks_before_max(t, b):
            return MAX_BANKS * t + KEY_BANKS * (b + 1)

        def blocks_attended(b, par):
            return b + 1 if par == 0 else b

        block = stack.enter_context(nc.Block())

        def rounds(eng, one_round):
            one_round(0, 0, 0, False, True)
            with eng.Fori(0, (BLOCKS - 2) // 2) as i:
                one_round(2 * i + 1, i + 1, 1, True, True)
                one_round(2 * i + 2, i + 1, 0, True, True)
            one_round(BLOCKS - 1, B, 1, True, False)

        @block.sync
        def _(sp):
            def load_x(t, par):
                wait(sp, xb_ready, t - 1)
                wait(sp, xn1_ready, t - 1)
                sp.dma_start(x_in[:, par], x_rows[t]).then_inc(x_in_landed[par], 16)

            def load_context(b):
                if not (isinstance(b, int) and b == 0):
                    wait(sp, b_ready, banks_before_max(2 * b - 2, b - 1) - KEY_BANKS + 2)
                sp.dma_start(cx[:, :, 0:M], context[b]).then_inc(cx_in, 16)

            def copy_keys(b):
                wait(sp, b_read, banks_before_max(2 * b, b))
                wait(sp, o_ready, GROUPS * 2 * b)
                sp.dma_start(kb[0:ROWS, 1].bitcast(F32), kb[0:ROWS, 0].bitcast(F32)).then_inc(keys_odd, 16)
                sp.dma_start(kr[0:ROWS, 1].bitcast(F32), kr[0:ROWS, 0].bitcast(F32)).then_inc(keys_odd, 16)
                sp.dma_start(vm[:, 1], vm[:, 0]).then_inc(keys_odd, 16)
                sp.dma_start(vr[:, 1], vr[:, 0]).then_inc(keys_odd, 16)

            def stack_queries(t, par):
                wait(sp, a_ready, 5 * GROUPS * (t - 1))
                wait(sp, qh_ready, KC * (t + 1))
                for row, src in ((ROW_HI, qh), (ROW_HI2, qh), (ROW_LO, ql)):
                    if src is ql:
                        wait(sp, ql_ready, KC * (t + 1))
                    for r in range(4):
                        sp.dma_start(xq[row:row + 32, par, r:G:4, :].bitcast(F32),
                                     src[32 * r:32 * r + 32, :, :]).then_inc(stacked[par], 16)

            def place_maxima(t, par):
                wait(sp, ct_copied, t + 1)
                for g in range(G):
                    sp.dma_start(xq[ROW_MAX:ROWS, par, g, :].bitcast(F32),
                                 ct[4 * g:4 * g + 4, :]).then_inc(max_placed[par], 16)

            def store(t):
                wait(sp, out_ready, 2 * (t + 1))
                sp.dma_start(out_rows[t], rt[:, :, :]).then_inc(stored, 16)

            def one_round(t, b, par, finish, prepare):
                if prepare:
                    if par == 1:
                        load_context(b)
                    load_x(t + 1, 1 - par)
                if par == 0:
                    copy_keys(b)
                if prepare:
                    stack_queries(t + 1, 1 - par)
                    place_maxima(t + 1, 1 - par)
                if finish:
                    store(t - 1)

            sp.dma_start(aux_sb[:, :], aux).then_inc(aux_in, 16)
            sp.dma_start(w[:, :, 0:3, :], weights[:, :, 0:3, :]).then_inc(w_in, 16)
            load_x(0, 0)
            sp.wait_ge(zeroed, 1)
            load_context(0)
            sp.dma_start(w[:, :, 3:NW, :], weights[:, :, 3:NW, :]).then_inc(w_rest_in, 16)
            stack_queries(0, 0)
            place_maxima(0, 0)
            rounds(sp, one_round)
            store(BLOCKS - 1)
            sp.wait_ge(stored, 16 * BLOCKS)

        @block.tensor
        def _(pe):
            reader = [None, None]

            def free(hf):
                if reader[hf]:
                    wait(pe, *reader[hf])

            def transpose_tiles(src, hf, done):
                for j in range(J):
                    last = pe.transpose(ps_w[:, hf, P * j:P * j + P], src[:, j, P * hf:P * hf + P], ident)
                last.then_inc(done, 1)

            def project_rows(src, weight, hf, done):
                for j in (2 * hf, 2 * hf + 1):
                    for kc in range(KC):
                        last = pe.matmul(ps_w[:, hf, C * (j % 2):C * (j % 2) + C], src[:, kc, P * j:P * j + P],
                                         w[:, kc, weight, :], start=(kc == 0), stop=(kc == KC - 1))
                last.then_inc(done, 1)

            def x1_transposed(t):
                pe.wait_ge(xn1_ready, t + 1)
                for hf in range(2):
                    free(hf)
                    transpose_tiles(xn, hf, x1t_ready)
                    reader[hf] = (x1t_copied, 2 * t + hf + 1)

            def queries(t):
                pe.wait_ge(x1t_copied, 2 * (t + 1))
                for hf in range(2):
                    free(hf)
                    project_rows(x1t, WQ, hf, q_ready)
                    reader[hf] = (qn_ready, 2 * t + hf + 1)

            def q_transposed(t):
                pe.wait_ge(qn_ready, 2 * (t + 1))
                for hf in range(2):
                    free(hf)
                    transpose_tiles(qn, hf, qt_ready)
                    reader[hf] = (ql_ready, 2 * t + hf + 1)

            def keys(b):
                pe.wait_ge(cx_in, 16 * (b + 1))
                u = banks_before_max(2 * b, b) - KEY_BANKS
                for ch in range(2):
                    wait(pe, b_read, u + ch - 1)
                    for kc in range(KC):
                        last = pe.matmul(ps_b[:, ch, :], cx[:, kc, P * ch:P * ch + P],
                                         w[:, kc, WK:WV + 1, :].rearrange("p a b -> p (a b)"),
                                         start=(kc == 0), stop=(kc == KC - 1))
                    last.then_inc(b_ready, 1)

            def keys_transposed(b):
                u = banks_before_max(2 * b, b) - KEY_BANKS
                pe.wait_ge(ks_ready, b + 1)
                for n in range(2, 6):
                    wait(pe, b_read, u + n - 1)
                    for h in range(4):
                        last = pe.transpose(ps_b[0:ROWS, n % 2, P * h:P * h + P],
                                            ks[:, 0, 2 * (n - 2) + h // 2, h % 2, :], ident)
                    last.then_inc(b_ready, 1)
                for n in range(6, 8):
                    wait(pe, b_read, u + n - 1)
                    for h in range(8):
                        last = pe.matmul(ps_b[0:ROWS, n % 2, SLOT * h:SLOT * h + M1],
                                         ks[0:M1, 1, 4 * (n - 6) + h // 2, h % 2, :],
                                         aux_sb[0:M1, AUX_ID:AUX_ID + M1], start=True, stop=True)
                    last.then_inc(b_ready, 1)

            def score_tile(t, b, par, j):
                u = banks_before_max(t, b) + G * j
                if j == 0:
                    pe.wait_ge(b_read, u)
                    pe.wait_ge(stacked[par], 16 * 12 * (b + 1))
                    if par == 1:
                        pe.wait_ge(keys_odd, 64 * (b + 1))
                for g in range(G):
                    pe.wait_ge(b_read, u + g - 1)
                    pe.matmul(ps_b[:, g % 2, 0:2 * M].rearrange("p (a m) -> p a m", a=2),
                              xq[0:ROW_MAX, par, g, P * j:P * j + P], kb[0:ROW_MAX, par, g, :, 0:M],
                              start=True, stop=True).then_inc(b_ready, 1)

            def maxima_transposed(t):
                pe.wait_ge(cs_ready, t + 1)
                free(0)
                for j in range(J):
                    last = pe.transpose(ps_w[0:4 * G, 0, P * j:P * j + P],
                                        cs[:, j].rearrange("p g q -> p (g q)"), ident)
                last.then_inc(ct_ready, 1)
                reader[0] = (ct_copied, t + 1)

            def attend_unit(t, b, par, n):
                gr, k = n // 5, n % 5
                if n == 0:
                    pe.wait_ge(max_placed[par], 128 * blocks_attended(b, par))
                wait(pe, e_ready, 20 * t + ((-1, 0, -2)[n] if n < 3 else n - 2))
                if k < 4:
                    h = 4 * gr + k
                    last = pe.matmul(ps_a[:, n % 3, :], kb[0:ROWS, par, h // 2, h % 2, 0:M0],
                                     xq[0:ROWS, par, h // 2, :], start=True, stop=True)
                else:
                    for g in (2 * gr, 2 * gr + 1):
                        last = pe.matmul(ps_a[:, n % 3, :], kr[0:ROWS, par, g, :], xq[0:ROWS, par, g, :],
                                         start=(g == 2 * gr), stop=(g == 2 * gr + 1))
                last.then_inc(a_ready, 1)

            def weigh_values(t, par, gr):
                pe.wait_ge(e_ready, 20 * t + 5 * gr + 5)
                wait(pe, on_ready, 4 * t + gr)
                pe.matmul(ps_o[:, :], vr[:, par, gr, :], e[:, (5 * gr + 4) % 10, :], start=True, stop=False,
                          skip_group_check=True)
                for k in range(4):
                    last = pe.matmul(ps_o[SLOT * k:SLOT * k + SLOT, :], vm[:, par, 4 * gr + k, :],
                                     e[:, (5 * gr + k) % 10, :], start=False, stop=True,
                                     skip_group_check=True)
                last.then_inc(o_ready, 1)

            def values_transposed(t, gr):
                pe.wait_ge(o_copied, 4 * t + gr + 1)
                for j in range(J):
                    last = pe.transpose(ps_o[:, P * j:P * j + P], osb[:, gr % 2, P * j:P * j + P], ident)
                last.then_inc(on_t_ready, 1)

            def o_transposed(t):
                pe.wait_ge(on_ready, 4 * (t + 1))
                for hf in range(2):
                    free(hf)
                    transpose_tiles(on, hf, ot_ready)
                    reader[hf] = (ot_copied, 2 * t + hf + 1)

            def out_projection(t):
                pe.wait_ge(ot_copied, 2 * (t + 1))
                for hf in range(2):
                    free(hf)
                    project_rows(ot, WP, hf, y_ready)
                    reader[hf] = (x2_ready, 2 * t + hf + 1)

            def x2_transposed(t):
                pe.wait_ge(xn2_ready, t + 1)
                for hf in range(2):
                    free(hf)
                    transpose_tiles(xn, hf, x2t_ready)
                    reader[hf] = (x2t_copied, 2 * t + hf + 1)

            def ffn_keys(t):
                pe.wait_ge(xk_ready, 2 * (t + 1))
                for hf in range(2):
                    free(hf)
                    for kc in range(KC):
                        last = pe.matmul(ps_w[:, hf, :], w[:, kc, FK, P * hf:P * hf + P], xk[:, kc, :],
                                         start=(kc == 0), stop=(kc == KC - 1))
                    last.then_inc(k2_ready, 1)
                    reader[hf] = (kact_ready, 2 * t + hf + 1)

            def ffn_gate(t):
                pe.wait_ge(xr_ready, 2 * (t + 1))
                for hf in range(2):
                    free(hf)
                    project_rows(xr, FR, hf, r_ready)
                    reader[hf] = (gate_ready, 2 * t + hf + 1)

            def ffn_values(t):
                pe.wait_ge(kact_ready, 2 * (t + 1))
                for hf in range(2):
                    free(hf)
                    project_rows(xd, FV, hf, kv2_ready)
                    reader[hf] = (gated, 2 * t + hf + 1)

            def one_round(t, b, par, finish, prepare):
                def attend(first, last):
                    for n in range(first, last + 1):
                        attend_unit(t, b, par, n)

                reader[0], reader[1] = (ct_copied, t + 1), (gated, 2 * t - 2)
                if finish:
                    o_transposed(t - 1)
                attend(0, 2)
                if finish:
                    out_projection(t - 1)
                if prepare:
                    x1_transposed(t + 1)
                attend(3, 4)
                if prepare:
                    queries(t + 1)
                    if par == 1:
                        keys(b)
                attend(5, 7)
                weigh_values(t, par, 0)
                attend(8, 9)
                values_transposed(t, 0)
                if finish:
                    x2_transposed(t - 1)
                if prepare:
                    q_transposed(t + 1)
                weigh_values(t, par, 1)
                attend(10, 12)
                if prepare and par == 1:
                    keys_transposed(b)
                values_transposed(t, 1)
                if finish:
                    ffn_keys(t - 1)
                attend(13, 14)
                if prepare:
                    score_tile(t + 1, b, 1 - par, 0)
                    score_tile(t + 1, b, 1 - par, 1)
                weigh_values(t, par, 2)
                if finish:
                    ffn_gate(t - 1)
                attend(15, 17)
                values_transposed(t, 2)
                if prepare:
                    score_tile(t + 1, b, 1 - par, 2)
                    score_tile(t + 1, b, 1 - par, 3)
                attend(18, 19)
                if finish:
                    ffn_values(t - 1)
                if prepare:
                    maxima_transposed(t + 1)
                weigh_values(t, par, 3)
                values_transposed(t, 3)

            pe.wait_ge(aux_in, 16)
            pe.wait_ge(centred, 1)
            keys(0)
            x1_transposed(0)
            queries(0)
            q_transposed(0)
            keys_transposed(0)
            for j in range(J):
                score_tile(0, 0, 0, j)
            maxima_transposed(0)
            pe.wait_ge(w_rest_in, 16)
            rounds(pe, one_round)
            last = BLOCKS - 1
            reader[0], reader[1] = (gated, 2 * last - 1), (gated, 2 * last)
            o_transposed(last)
            out_projection(last)
            x2_transposed(last)
            ffn_keys(last)
            ffn_gate(last)
            ffn_values(last)

        @block.scalar
        def _(act):
            def x1_copy(t):
                wait(act, q_ready, 2 * t)
                for hf in range(2):
                    act.wait_ge(x1t_ready, 2 * t + hf + 1)
                    nc.scalar.activation(x1t[:, hf, :], ps_w[:, hf, :], ACT.Copy).then_inc(x1t_copied, 1)

            def q_square(t, b, par):
                wait(act, stacked[1 - par], 192 * stacks_before(b, par))
                for hf in range(2):
                    act.wait_ge(q_ready, 2 * t + hf + 1)
                    nc.scalar.activation(ql[:, hf, :], ps_w[:, hf, :], ACT.Square).then_inc(q_squared, 1)

            def q_high(t):
                for hf in range(2):
                    act.wait_ge(qt_ready, 2 * t + hf + 1)
                    nc.scalar.activation(qh[:, hf, :].bitcast(F32R), ps_w[:, hf, :],
                                         ACT.Copy).then_inc(qh_ready, 1)

            def maxima_copy(t, b, par):
                wait(act, max_placed[1 - par], 128 * stacks_before(b, par))
                act.wait_ge(ct_ready, t + 1)
                nc.scalar.activation(ct[:, :], ps_w[0:4 * G, 0, :], ACT.Copy).then_inc(ct_copied, 1)

            def stacks_before(b, par):
                return b if par == 0 else b + 1

            def exponentials(t, first, last):
                for n in range(first, last + 1):
                    wait(act, o_ready, 4 * t + n // 5 - 1)
                    act.wait_ge(a_ready, 20 * t + n + 1)
                    nc.scalar.activation(e[:, n % 10, :], ps_a[:, n % 3, :], ACT.Exp).then_inc(e_ready, 1)

            def o_copy(t, gr):
                wait(act, on_t_ready, 4 * t + gr - 1)
                act.wait_ge(o_ready, 4 * t + gr + 1)
                nc.scalar.activation(osb[:, gr % 2, :], ps_o[:, :], ACT.Copy).then_inc(o_copied, 1)

            def on_copy(t):
                wait(act, y_ready, 2 * t)
                for hf in range(2):
                    act.wait_ge(ot_ready, 2 * t + hf + 1)
                    nc.scalar.activation(ot[:, hf, :], ps_w[:, hf, :], ACT.Copy).then_inc(ot_copied, 1)

            def x2_copy(t, par):
                wait(act, xk_ready, 2 * t)
                for hf in range(2):
                    act.wait_ge(x2t_ready, 2 * t + hf + 1)
                    if par == 0:
                        nc.scalar.activation(x2t[:, 1, hf, 0:1], ps_w[:, hf, T - 1:T], ACT.Copy)
                    nc.scalar.activation(x2t[:, par, hf, 1:T + 1], ps_w[:, hf, :],
                                         ACT.Copy).then_inc(x2t_copied, 1)

            def ffn_relu(t):
                for hf in range(2):
                    act.wait_ge(k2_ready, 2 * t + hf + 1)
                    nc.scalar.activation(xd[:, hf, :], ps_w[:, hf, :], ACT.Relu).then_inc(relu_ready, 1)

            def ffn_tanh(t):
                wait(act, stored, 16 * t)
                for hf in range(2):
                    act.wait_ge(r_ready, 2 * t + hf + 1)
                    nc.scalar.activation(rt[:, 2 * hf:2 * hf + 2, :].rearrange("p j c -> p (j c)"),
                                         ps_w[:, hf, :], ACT.Tanh, scale=0.5).then_inc(gate_ready, 1)

            def one_round(t, b, par, finish, prepare):
                if finish:
                    on_copy(t - 1)
                exponentials(t, 0, 2)
                if prepare:
                    x1_copy(t + 1)
                exponentials(t, 3, 4)
                if prepare:
                    q_square(t + 1, b, 1 - par)
                exponentials(t, 5, 7)
                o_copy(t, 0)
                exponentials(t, 8, 9)
                if finish:
                    x2_copy(t - 1, 1 - par)
                if prepare:
                    q_high(t + 1)
                o_copy(t, 1)
                exponentials(t, 10, 12)
                if finish:
                    ffn_relu(t - 1)
                exponentials(t, 13, 14)
                o_copy(t, 2)
                if finish:
                    ffn_tanh(t - 1)
                exponentials(t, 15, 19)
                if prepare:
                    maxima_copy(t + 1, b, 1 - par)
                o_copy(t, 3)

            x1_copy(0)
            q_square(0, 0, 0)
            q_high(0)
            maxima_copy(0, 0, 0)
            rounds(act, one_round)
            last = BLOCKS - 1
            on_copy(last)
            x2_copy(last, 1)
            ffn_relu(last)
            ffn_tanh(last)

        @block.vector
        def _(dve):
            Q_STEPS, K_STEPS, X_STEPS = 13, 22, 2

            def heads(ap):
                return ap.rearrange("p (h d) -> p h d", d=D)

            def spread(ap, n):
                return ap.unsqueeze(2).broadcast_to([P, n, D])

            def rsqrt_of_variance(steps, buf):
                v, h, y, a, squares = (buf[:, n, :] for n in range(5))
                steps.then(dve.tensor_scalar(v, squares, 1.0 / D, EPS, ALU.mult, ALU.add))
                steps.then(dve.tensor_scalar(h, v, -0.5, None, ALU.mult))
                steps.then(dve.tensor_scalar(y.bitcast(I32), v.bitcast(I32), -0.5, float(0x5F3759DF),
                                             ALU.mult, ALU.add))
                for _ in range(3):
                    steps.then(dve.tensor_tensor(a, y, y, ALU.mult))
                    steps.then(dve.tensor_tensor(a, a, h, ALU.mult))
                    steps.then(dve.scalar_tensor_tensor(y, a, 1.5, y, ALU.add, ALU.mult))

            def row_statistics(which, t, src, done):
                steps = Steps(dve, ln_steps[which], t)
                for j in range(J):
                    last = dve.bn_stats(st[:, which, j, :], src[:, j, :])
                steps.then(last)
                wait(dve, (rs1_ready, rs2_ready)[which], t)
                dve.memset(spare[:, :], 0.0)
                for j in range(J):
                    last = dve.bn_aggr(mv[:, which, j, :], st[:, which, j, :])
                last.then_inc(done, 1)

            def normalize_rows(which, src, done):
                for j in range(J):
                    last = dve.tensor_scalar(xn[:, j, :], src[:, j, :], mv[:, which, j, 0:1],
                                             rs[:, which, j:j + 1], ALU.subtract, ALU.mult)
                last.then_inc(done, 1)

            def norm1(t, b, par):
                dve.wait_ge(x_in_landed[par], 16 * (b + 1))
                row_statistics(0, t, x_in[:, par], mv1_ready)
                dve.wait_ge(rs1_ready, t + 1)
                wait(dve, x2t_ready, 2 * (t - 2))
                wait(dve, x1t_ready, 2 * t)
                normalize_rows(0, x_in[:, par], xn1_ready)

            def norm2_statistics(t):
                dve.wait_ge(x2_ready, 2 * (t + 1))
                row_statistics(1, t, x2, mv2_ready)

            def norm2(t):
                dve.wait_ge(rs2_ready, t + 1)
                dve.wait_ge(x1t_ready, 2 * (min(t + 3, BLOCKS) if isinstance(t, int) else t + 3))
                wait(dve, x2t_ready, 2 * t)
                normalize_rows(1, x2, xn2_ready)

            def queries(t):
                steps = Steps(dve, q_steps, Q_STEPS * t)
                dve.wait_ge(q_squared, 2 * (t + 1))
                steps.then(dve.tensor_reduce(qst[:, 4, :], ql[:, :, :].rearrange("p a (h d) -> p (a h) d", d=D),
                                             AX_X, ALU.add))
                rsqrt_of_variance(steps, qst)
                wait(dve, qt_ready, 2 * t)
                for hf in range(2):
                    dve.tensor_tensor(heads(qn[:, 2 * hf:2 * hf + 2, :].rearrange("p j c -> p (j c)")),
                                      heads(ps_w[:, hf, :]),
                                      spread(qst[:, 2, 2 * H * hf:2 * H * hf + 2 * H], 2 * H),
                                      ALU.mult).then_inc(qn_ready, 1)
                assert steps.n == Q_STEPS

            def q_low(t):
                for hf in range(2):
                    dve.wait_ge(qh_ready, 2 * t + hf + 1)
                    dve.tensor_tensor(ql[:, hf, :].bitcast(F32R), ps_w[:, hf, :], qh[:, hf, :],
                                      ALU.subtract).then_inc(ql_ready, 1)

            def keys(b):
                steps = Steps(dve, k_steps, K_STEPS * b)
                u = banks_before_max(2 * b, b) - KEY_BANKS
                g, bb = (aux_sb[:, a:a + D].unsqueeze(1).broadcast_to([P, 2 * H, D]) for a in (AUX_G, AUX_B))
                gsc, bsc = (gs[:, n, :].unsqueeze(1).broadcast_to([P, 2 * H, D]) for n in range(2))
                kh, kth = (t_[:, :, :].rearrange("p a (h d) -> p (a h) d", d=D) for t_ in (kf, kt))
                dve.wait_ge(b_ready, u + 2)
                steps.then(dve.tensor_copy(kf[:, :, :], ps_b[:, :, 0:C]))
                wait(dve, o_ready, GROUPS * (2 * b - 1))
                wait(dve, keys_odd, 64 * b)
                dve.tensor_copy(vm[:, 0, :, 0:D], heads(ps_b[:, 0, C:2 * C]))
                for k in range(4):
                    last = dve.tensor_copy(
                        vr[SLOT * k:SLOT * k + M1, 0, :, SLOT * k:SLOT * k + D],
                        ps_b[0:M1, 1, C:2 * C].rearrange("p (a k d) -> p a k d", k=4, d=D)[:, :, k, :])
                last.then_inc(b_read, 2)
                steps.then(dve.tensor_tensor(kt[:, :, :], kf[:, :, :], kf[:, :, :], ALU.mult))
                steps.then(dve.tensor_reduce(kst[:, 4, :], kth, AX_X, ALU.add))
                rsqrt_of_variance(steps, kst)
                steps.then(dve.tensor_tensor(kh, kh, spread(kst[:, 2, :], 2 * H), ALU.mult))
                steps.then(dve.tensor_tensor(kh, kh, g, ALU.mult))
                steps.then(dve.tensor_tensor(kh, kh, bb, ALU.add))
                steps.then(dve.tensor_tensor(kth, kh, bsc, ALU.mult))
                steps.then(dve.tensor_reduce(kst[:, 4, :], kth, AX_X, ALU.add))
                steps.then(dve.tensor_tensor(kth, kh, gsc, ALU.mult))

                def rows(j, first, n):
                    return ks[:, :, :, j, first:first + n].rearrange("p a g n -> p (a g) n")

                def of_head(ap, j):
                    return ap.rearrange("p (g j) n -> p g j n", j=2)[:, :, j, :]

                const = kst[:, 4, :].unsqueeze(2)
                for j in range(2):
                    for row in (ROW_HI, ROW_LO):
                        dve.tensor_copy(rows(j, row + D * j, D).bitcast(F32R), of_head(kth, j))
                    last = dve.tensor_copy(rows(j, ROW_ONE, 1).bitcast(F32R), of_head(const, j))
                steps.then(last)
                for j in range(2):
                    dve.tensor_tensor(rows(j, ROW_HI2 + D * j, D).bitcast(F32R), of_head(kth, j),
                                      rows(j, ROW_HI + D * j, D), ALU.subtract)
                    last = dve.tensor_tensor(rows(j, ROW_ONE + 1, 1).bitcast(F32R), of_head(const, j),
                                             rows(j, ROW_ONE, 1), ALU.subtract)
                last.then_inc(ks_ready, 1)
                assert steps.n == K_STEPS

            def keys_stacked(b):
                u = banks_before_max(2 * b, b) - KEY_BANKS
                wait(dve, a_ready, 20 * (2 * b - 1))
                for n in range(2, 6):
                    dve.wait_ge(b_ready, u + n + 1)
                    g = 2 * (n - 2)
                    dve.tensor_copy(kb[0:ROWS, 0, g:g + 2, :, 0:M0].rearrange("p g j m -> p (g j) m"),
                                    ps_b[0:ROWS, n % 2, :].rearrange("p (h m) -> p h m", m=P)).then_inc(b_read, 1)
                for n in range(6, 8):
                    dve.wait_ge(b_ready, u + n + 1)
                    g = 4 * (n - 6)
                    rest = ps_b[0:ROWS, n % 2, 0:8 * SLOT].rearrange("p (g j m) -> p g j m", g=4, j=2)
                    dve.tensor_copy(kb[0:ROWS, 0, g:g + 4, :, M0:M].rearrange("p g j m -> p (g j) m"),
                                    ps_b[0:ROWS, n % 2, 0:8 * SLOT].rearrange("p (h m) -> p h m", m=SLOT)[:, :, 0:M1])
                    for odd in range(2):
                        slots = kr[0:ROWS, 0, g + odd:g + 4:2, 2 * SLOT * odd:2 * SLOT * odd + 2 * SLOT]
                        last = dve.tensor_copy(slots.rearrange("p g (j m) -> p g j m", j=2)[:, :, :, 0:M1],
                                               rest[:, odd:4:2, :, 0:M1])
                    last.then_inc(b_read, 1)

            def maxima(t, b, j):
                u = banks_before_max(t, b) + G * j
                for g in range(G):
                    dve.wait_ge(b_ready, u + g + 1)
                    dve.tensor_reduce(nmax[:, j, 2 * g:2 * g + 2],
                                      ps_b[:, g % 2, 0:2 * M].rearrange("p (a m) -> p a m", a=2),
                                      AX_X, ALU.max, negate=True).then_inc(b_read, 1)

            def maxima_split(t, b):
                dve.wait_ge(b_read, banks_before_max(t, b) + MAX_BANKS)
                wait(dve, ct_ready, t)
                by_head = nmax[:, :, :].rearrange("p j (g a) -> p j g a", a=2)
                for a in range(2):
                    last = dve.tensor_copy(cs[:, :, :, 2 * a].bitcast(F32R), by_head[:, :, :, a])
                last.then_inc(c_steps, 1)
                dve.wait_ge(c_steps, t + 1)
                for a in range(2):
                    last = dve.tensor_tensor(cs[:, :, :, 2 * a + 1].bitcast(F32R), by_head[:, :, :, a],
                                             cs[:, :, :, 2 * a], ALU.subtract)
                last.then_inc(cs_ready, 1)

            def divide(t, gr):
                dve.wait_ge(on_t_ready, 4 * t + gr + 1)
                by_slot = ps_o[:, :].rearrange("p (j k d) -> p j k d", k=4, d=SLOT)
                dve.reciprocal(rl[:, :, :], by_slot[:, :, :, D]).then_inc(o_steps, 1)
                dve.wait_ge(o_steps, 4 * t + gr + 1)
                wait(dve, ot_ready, 2 * t)
                dve.tensor_tensor(on[:, :, 4 * D * gr:4 * D * gr + 4 * D].rearrange("p j (k d) -> p j k d", d=D),
                                  by_slot[:, :, :, 0:D], rl[:, :, :].unsqueeze(3).broadcast_to([P, J, 4, D]),
                                  ALU.mult).then_inc(on_ready, 1)

            def residual(t, par):
                dve.wait_ge(xb_ready, t + 1)
                for hf in range(2):
                    dve.wait_ge(y_ready, 2 * t + hf + 1)
                    dve.tensor_tensor(x2[:, 2 * hf:2 * hf + 2, :].rearrange("p j c -> p (j c)"), ps_w[:, hf, :],
                                      xb[:, par, 2 * hf:2 * hf + 2, :].rearrange("p j c -> p (j c)"),
                                      ALU.add).then_inc(x2_ready, 1)

            def mix(t, par):
                steps = Steps(dve, xd_ready, X_STEPS * t)
                wait(dve, kv2_ready, 2 * t)
                wait(dve, r_ready, 2 * t)
                wait(dve, k2_ready, 2 * t)
                for hf in range(2):
                    dve.wait_ge(x2t_copied, 2 * t + hf + 1)
                    now, before = x2t[:, par, hf, 1:T + 1], x2t[:, par, hf, 0:T]
                    steps.then(dve.tensor_tensor(xd[:, hf, :], now, before, ALU.subtract))
                    dve.scalar_tensor_tensor(xr[:, hf, :], xd[:, hf, :], aux_sb[:, AUX_MU_R + hf:AUX_MU_R + hf + 1],
                                             before, ALU.mult, ALU.add).then_inc(xr_ready, 1)
                    dve.scalar_tensor_tensor(xk[:, hf, :], xd[:, hf, :], aux_sb[:, AUX_MU_K + hf:AUX_MU_K + hf + 1],
                                             before, ALU.mult, ALU.add).then_inc(xk_ready, 1)

            def ffn_square(t):
                for hf in range(2):
                    dve.wait_ge(relu_ready, 2 * t + hf + 1)
                    dve.tensor_tensor(xd[:, hf, :], ps_w[:, hf, :], xd[:, hf, :], ALU.mult).then_inc(kact_ready, 1)

            def combine(t):
                dve.wait_ge(gate_ready, 2 * (t + 1))
                for hf in range(2):
                    dve.wait_ge(kv2_ready, 2 * t + hf + 1)
                    half = rt[:, 2 * hf:2 * hf + 2, :].rearrange("p j c -> p (j c)")
                    dve.scalar_tensor_tensor(half, half, 1.0, ps_w[:, hf, :], ALU.add, ALU.mult).then_inc(gated, 1)
                for hf in range(2):
                    dve.wait_ge(gated, 2 * t + hf + 1)
                    half = rt[:, 2 * hf:2 * hf + 2, :].rearrange("p j c -> p (j c)")
                    dve.scalar_tensor_tensor(half, half, 0.5, x2[:, 2 * hf:2 * hf + 2, :].rearrange("p j c -> p (j c)"),
                                             ALU.mult, ALU.add).then_inc(out_ready, 1)

            def one_round(t, b, par, finish, prepare):
                if prepare:
                    norm1(t + 1, b, 1 - par)
                if finish:
                    residual(t - 1, 1 - par)
                    norm2_statistics(t - 1)
                if prepare:
                    queries(t + 1)
                if finish:
                    norm2(t - 1)
                if prepare and par == 1:
                    keys(b)
                divide(t, 0)
                if prepare:
                    q_low(t + 1)
                if finish:
                    mix(t - 1, 1 - par)
                if prepare and par == 1:
                    keys_stacked(b)
                divide(t, 1)
                if finish:
                    ffn_square(t - 1)
                if prepare:
                    maxima(t + 1, b, 0)
                    maxima(t + 1, b, 1)
                divide(t, 2)
                if prepare:
                    maxima(t + 1, b, 2)
                    maxima(t + 1, b, 3)
                    maxima_split(t + 1, b)
                if finish:
                    combine(t - 1)
                divide(t, 3)

            dve.wait_ge(w_in, 16)
            for n, weight in enumerate((WK, WQ)):
                for kc in range(KC):
                    last = dve.tensor_reduce(wsum[:, n, kc, :], heads(w[:, kc, weight, :]), AX_X, ALU.add)
            last.then_inc(w_steps, 1)
            dve.wait_ge(w_steps, 1)
            for n, weight in enumerate((WK, WQ)):
                for kc in range(KC):
                    last = dve.scalar_tensor_tensor(heads(w[:, kc, weight, :]), spread(wsum[:, n, kc, :], H), -1.0 / D,
                                                    heads(w[:, kc, weight, :]), ALU.mult, ALU.add)
            last.then_inc(centred, 1)
            dve.wait_ge(aux_in, 16)
            dve.tensor_scalar(gs[:, 0, :], aux_sb[:, AUX_G:AUX_G + D], SCALE, None, ALU.mult)
            dve.tensor_scalar(gs[:, 1, :], aux_sb[:, AUX_B:AUX_B + D], SCALE, None, ALU.mult).then_inc(w_steps, 1)
            dve.wait_ge(w_steps, 2)
            dve.memset(ks[:, :, :, :, :], 0.0).then_inc(w_steps, 1)
            dve.memset(xq[ROW_ONE:ROW_MAX, 0].bitcast(F32), 1.0)
            dve.memset(kb[:, 0].bitcast(F32), 0.0)
            dve.wait_ge(w_steps, 3)
            for j in range(2):
                last = dve.memset(ks[:, :, :, j, ROW_MAX + 2 * j:ROW_MAX + 2 * j + 2], 1.0)
            last.then_inc(w_steps, 1)
            dve.wait_ge(w_steps, 4)
            dve.wait_ge(zeroed, ZEROED)
            norm1(0, 0, 0)
            keys(0)
            queries(0)
            q_low(0)
            keys_stacked(0)
            for j in range(J):
                maxima(0, 0, j)
            maxima_split(0, 0)
            rounds(dve, one_round)
            last = BLOCKS - 1
            residual(last, 1)
            norm2_statistics(last)
            norm2(last)
            mix(last, 1)
            ffn_square(last)
            combine(last)

        @block.gpsimd
        def _(pool):
            def rstd(which, t, ready, done, steps_sem):
                pool.wait_ge(ready, t + 1)
                steps = Steps(pool, steps_sem, t)
                wait(pool, (xn1_ready, xn2_ready)[which], t)
                steps.then(pool.tensor_tensor(ve[:, which, :], mv[:, which, :, 1], eps[:, :], ALU.add))
                pool.tensor_tensor(rs[:, which, :], ve[:, which, :], minus_half[:, :], ALU.pow).then_inc(done, 1)

            def with_bias(t, b, par):
                wait(pool, x2_ready, 2 * (t - 1))
                pool.wait_ge(x_in_landed[par], 16 * (b + 1))
                pool.tensor_tensor(xb[:, par], x_in[:, par],
                                   aux_sb[:, AUX_BP:AUX_BP + C].unsqueeze(1).broadcast_to([P, J, C]),
                                   ALU.add).then_inc(xb_ready, 1)

            def one_round(t, b, par, finish, prepare):
                if prepare:
                    rstd(0, t + 1, mv1_ready, rs1_ready, p_steps)
                if finish:
                    rstd(1, t - 1, mv2_ready, rs2_ready, carried)
                if prepare:
                    with_bias(t + 1, b, 1 - par)

            steps = Steps(pool, zeroed, 0)
            steps.then(pool.memset(cx[:, :, M:2 * P], 0.0))
            steps.then(pool.memset(eps[:, :], EPS))
            steps.then(pool.memset(minus_half[:, :], -0.5))
            steps.then(pool.memset(vm[:, 0], 0.0))
            steps.then(pool.memset(vm[:, 0, :, D:D + 1], 1.0))
            steps.then(pool.memset(vr[:, 0], 0.0))
            for k in range(4):
                steps.then(pool.memset(vr[SLOT * k:SLOT * k + M1, 0, :, SLOT * k + D:SLOT * k + D + 1], 1.0))
            steps.then(pool.memset(kr[:, 0].bitcast(F32), 0.0))
            steps.then(pool.memset(x2t[:, 0, :, 0:1], 0.0))
            steps.then(pool.memset(xq[ROW_ONE:ROW_MAX, 1].bitcast(F32), 1.0))
            assert steps.n == ZEROED
            pool.wait_ge(aux_in, 16)
            rstd(0, 0, mv1_ready, rs1_ready, p_steps)
            with_bias(0, 0, 0)
            rounds(pool, one_round)
            rstd(1, BLOCKS - 1, mv2_ready, rs2_ready, carried)


def kernel(x, ctx_1024, L0_xattn_Wq, L0_xattn_Wk, L0_xattn_Wv, L0_xattn_Wp, L0_xattn_bp, L0_xattn_ln_g,
           L0_xattn_ln_b, L0_ffn_W_r, L0_ffn_W_k, L0_ffn_W_v, L0_ffn_mu_r, L0_ffn_mu_k):
    import concourse.bacc as bacc
    from concourse.bass_utils import run_bass_kernel_spmd

    def spread(row):
        return np.broadcast_to(np.asarray(row)[None, :], (P, row.shape[0]))

    def column(vector):
        return np.asarray(vector).reshape(KC, P).T

    stacked = np.stack([np.asarray(m).T for m in (L0_xattn_Wk, L0_xattn_Wv, L0_xattn_Wq, L0_xattn_Wp,
                                                  L0_ffn_W_r, L0_ffn_W_k, L0_ffn_W_v)])
    arrays = {
        "x": np.ascontiguousarray(np.asarray(x).reshape(B * N, C)),
        "context": np.ascontiguousarray(np.asarray(ctx_1024).reshape(B, M, KC, P).transpose(0, 3, 2, 1)),
        "weights": np.ascontiguousarray(stacked.reshape(NW, KC, P, C).transpose(2, 1, 0, 3)),
        "aux": np.ascontiguousarray(np.concatenate(
            [column(L0_ffn_mu_r), column(L0_ffn_mu_k), spread(L0_xattn_ln_g), spread(L0_xattn_ln_b),
             spread(L0_xattn_bp), np.eye(P, dtype=np.float32)], axis=1)),
    }
    nc = bacc.Bacc("TRN2", target_bir_lowering=False, num_devices=1)
    args = [nc.dram_tensor(name, a.shape, mybir.dt.from_np(a.dtype), kind="ExternalInput").ap()
            for name, a in arrays.items()]
    out = nc.dram_tensor("out", (B * N, C), F32, kind="ExternalOutput").ap()
    xattn_ffn(nc, *args, out)
    result = run_bass_kernel_spmd(nc, [arrays], core_ids=[0])
    return result.results[0]["out"].reshape(B, N, C)
```

```python
from contextlib import ExitStack

import numpy as np

import concourse.bass as bass
from concourse import mybir

ALU = mybir.AluOpType
ACT = mybir.ActivationFunctionType
F32 = mybir.dt.float32
F32R = mybir.dt.float32r
I32 = mybir.dt.int32
AX_X = mybir.AxisListType.X

P = 128
B, N, C = 4, 1024, 256
M, H, D = 154, 16, 16
SCALE = 8.0 / D
EPS = 1e-5
T = 512
BLOCKS = B * N // T
J = T // P
KC = C // P
G = H // 2
GROUPS = H // 4
M0, M1 = P, M - P
SLOT = 32
KPAD = M + 6

ROW_HI, ROW_HI2, ROW_LO, ROW_ONE, ROW_MAX, ROWS = 0, 32, 64, 96, 98, 102
WQ, WK, WV, WP, FR, FK, FV = range(7)
NW = 7
AUX_MU_R, AUX_MU_K, AUX_G, AUX_B, AUX_BP, AUX_ID = 0, 2, 4, 20, 36, 36 + C
AUX = AUX_ID + P


def wait(eng, sem, value):
    if isinstance(value, int) and value <= 0:
        return
    eng.wait_ge(sem, value)


class Steps:

    def __init__(self, eng, sem, before):
        self.eng, self.sem, self.before, self.n = eng, sem, before, 0

    def then(self, ins):
        self.n += 1
        ins.then_inc(self.sem, 1)
        self.eng.wait_ge(self.sem, self.before + self.n)


def xattn_ffn(nc, x, context, weights, aux, out):
    x_rows = x.rearrange("(t j p) c -> t p j c", j=J, p=P)
    out_rows = out.rearrange("(t j p) c -> t p j c", j=J, p=P)

    with ExitStack() as stack:
        def sb(name, shape, dt=F32):
            return stack.enter_context(nc.sbuf_tensor(name, shape, dt))

        def ps(name, shape):
            return stack.enter_context(nc.psum_tensor(name, shape, F32))

        def sem(name):
            return stack.enter_context(nc.semaphore(name))

        w = sb("w", [P, KC, NW, C])
        aux_sb = sb("aux_sb", [P, AUX])
        ident = aux_sb[:, AUX_ID:AUX_ID + P]
        minus_half = sb("minus_half", [P, J])
        minus_one = sb("minus_one", [P, J])
        eps = sb("eps", [P, J])
        rest = sb("rest", [P, 2 * KC])
        spare = sb("spare", [P, 2])
        spare2 = sb("spare2", [P, 2])
        gs = sb("gs", [P, 2, D])
        wsum = sb("wsum", [P, 2, KC, H])
        cx = sb("cx", [P, KC, 2 * P])
        kb = sb("kb", [P, 2, G, 2, KPAD], F32R)
        kr = sb("kr", [P, 2, G, P], F32R)
        vm = sb("vm", [P, 2, H, SLOT])
        vr = sb("vr", [P, 2, GROUPS, P])
        ks = sb("ks", [P, 2, G, 2, ROWS])
        kf = sb("kf", [P, 2, C])
        kt = sb("kt", [P, 2, C])
        kc_sb = sb("kc_sb", [P, 2 * H])
        x_in = sb("x_in", [P, 2, J, C])
        st = sb("st", [P, 2, J, 6])
        mv = sb("mv", [P, 2, J, 2])
        ve = sb("ve", [P, 2, J])
        rs = sb("rs", [P, 2, J])
        nm = sb("nm", [P, 2, J])
        nb = sb("nb", [P, 2, J])
        xn = sb("xn", [P, J, C])
        x1t = sb("x1t", [P, KC, T])
        qn = sb("qn", [P, J, C])
        qst = sb("qst", [P, 5, (J + 2) * H])
        qh = sb("qh", [P, KC, T])
        ql = sb("ql", [P, KC, T])
        xq = sb("xq", [P, 2, G, T], F32R)
        nmax = sb("nmax", [P, J, 4])
        cs = sb("cs", [P, J, 2, 4])
        ct = sb("ct", [8, T])
        e = sb("e", [P, 10, T])
        osb = sb("osb", [P, T])
        rl = sb("rl", [P, J, 4])
        on = sb("on", [P, J, C])
        ot = sb("ot", [P, KC, T])
        xb = sb("xb", [P, 2, J, C])
        x2 = sb("x2", [P, J, C])
        x2t = sb("x2t", [P, 2, KC, T + 1])
        xd = sb("xd", [P, KC, T])
        xr = sb("xr", [P, KC, T])
        xk = sb("xk", [P, KC, T])
        rt = sb("rt", [P, J, C])

        ps_a = ps("ps_a", [P, 3, T])
        ps_b = ps("ps_b", [P, 2, T])
        ps_o = ps("ps_o", [P, T])
        ps_w = ps("ps_w", [P, 2, T])

        def sems(text):
            return [sem(name) for name in text.split()]

        aux_in, wq_in, wkv_in, w_rest_in, cx_in, x_landed, zeroed, centred, w_steps = sems(
            "aux_in wq_in wkv_in w_rest_in cx_in x_landed zeroed centred w_steps")
        kp_ready, kf_copied, v_copied, k_steps, ks_ready = sems("kp_ready kf_copied v_copied k_steps ks_ready")
        kt_ready, kt_copied, keys_odd = sems("kt_ready kt_copied keys_odd")
        mv1_ready, rs1_ready, xn1_ready, x1t_ready, x1t_copied = sems("mv1_ready rs1_ready xn1_ready x1t_ready x1t_copied")
        q_ready, q_squared, q_steps, qn_ready = sems("q_ready q_squared q_steps qn_ready")
        qt_ready, qh_ready, ql_ready, stacked = sems("qt_ready qh_ready ql_ready stacked")
        b_ready, b_read, c_steps, cs_ready, ct_ready, ct_copied = sems(
            "b_ready b_read c_steps cs_ready ct_ready ct_copied")
        max_placed = sems("max_placed0 max_placed1")
        a_ready, e_ready, o_ready, o_copied, on_t_ready, o_steps, on_ready = sems(
            "a_ready e_ready o_ready o_copied on_t_ready o_steps on_ready")
        ot_ready, ot_copied, y_ready, xb_ready, x2_ready = sems("ot_ready ot_copied y_ready xb_ready x2_ready")
        mv2_ready, rs2_ready, xn2_ready, x2t_ready, x2t_copied = sems("mv2_ready rs2_ready xn2_ready x2t_ready x2t_copied")
        ln1_steps, ln2_steps, p1_steps, p2_steps, xk_begun, xr_begun, xk_ready, xr_ready = sems(
            "ln1_steps ln2_steps p1_steps p2_steps xk_begun xr_begun xk_ready xr_ready")
        k2_ready, relu_ready, kact_ready = sems("k2_ready relu_ready kact_ready")
        r_ready, tanh_ready, gate_ready, kv2_ready, gated, out_ready, stored = sems(
            "r_ready tanh_ready gate_ready kv2_ready gated out_ready stored")

        ZEROED = 14
        UNITS = 2 * J
        EXPS = 5 * GROUPS

        block = stack.enter_context(nc.Block())

        def rounds(eng, one_round):
            one_round(0, 0, 0, False, True)
            with eng.Fori(0, (BLOCKS - 2) // 2) as i:
                one_round(2 * i + 1, i + 1, 1, True, True)
                one_round(2 * i + 2, i + 1, 0, True, True)
            one_round(BLOCKS - 1, B, 1, True, False)

        @block.sync
        def _(sp):
            def load_x(t, par):
                sp.dma_start(x_in[:, par], x_rows[t]).then_inc(x_landed, 16)

            def load_context(b):
                if not (isinstance(b, int) and b == 0):
                    wait(sp, kp_ready, 2 * b)
                sp.dma_start(cx[:, :, 0:M], context[b]).then_inc(cx_in, 16)

            def copy_keys(b):
                wait(sp, o_ready, GROUPS * 2 * b)
                sp.dma_start(kb[0:ROWS, 1].bitcast(F32), kb[0:ROWS, 0].bitcast(F32)).then_inc(keys_odd, 16)
                sp.dma_start(kr[0:ROWS, 1].bitcast(F32), kr[0:ROWS, 0].bitcast(F32)).then_inc(keys_odd, 16)
                sp.dma_start(vm[:, 1], vm[:, 0]).then_inc(keys_odd, 16)
                sp.dma_start(vr[:, 1], vr[:, 0]).then_inc(keys_odd, 16)

            def stack_queries(t, par):
                wait(sp, qh_ready, KC * (t + 1))
                for row, src in ((ROW_HI, qh), (ROW_HI2, qh), (ROW_LO, ql)):
                    if src is ql:
                        wait(sp, ql_ready, KC * (t + 1))
                    for r in range(4):
                        sp.dma_start(xq[row:row + 32, par, r:G:4, :].bitcast(F32),
                                     src[32 * r:32 * r + 32, :, :]).then_inc(stacked, 16)

            def place_maxima(t, par, gr):
                wait(sp, ct_copied, GROUPS * t + gr + 1)
                for g in range(2):
                    sp.dma_start(xq[ROW_MAX:ROWS, par, 2 * gr + g, :].bitcast(F32),
                                 ct[4 * g:4 * g + 4, :]).then_inc(max_placed[g], 16)

            def one_round(t, b, par, finish, prepare):
                if prepare:
                    load_x(t + 1, 1 - par)
                    if par == 1:
                        load_context(b)
                if par == 0:
                    copy_keys(b)
                place_maxima(t, par, 1)
                place_maxima(t, par, 2)
                if prepare:
                    stack_queries(t + 1, 1 - par)
                place_maxima(t, par, 3)
                if prepare:
                    place_maxima(t + 1, 1 - par, 0)

            load_x(0, 0)
            sp.dma_start(aux_sb[:, :], aux).then_inc(aux_in, 16)
            sp.wait_ge(zeroed, 1)
            load_context(0)
            stack_queries(0, 0)
            place_maxima(0, 0, 0)
            rounds(sp, one_round)

        @block.tensor
        def _(pe):
            reader = [[], []]

            def free(hf):
                for sem_, count in reader[hf]:
                    wait(pe, sem_, count)

            def transpose_tiles(src, hf, done):
                for j in range(J):
                    last = pe.transpose(ps_w[:, hf, P * j:P * j + P], src[:, j, P * hf:P * hf + P], ident)
                last.then_inc(done, 1)

            def project_rows(src, weight, hf, done):
                for j in (2 * hf, 2 * hf + 1):
                    for kc in range(KC):
                        last = pe.matmul(ps_w[:, hf, C * (j % 2):C * (j % 2) + C], src[:, kc, P * j:P * j + P],
                                         w[:, kc, weight, :], start=(kc == 0), stop=(kc == KC - 1))
                last.then_inc(done, 1)

            def x1_transposed(t):
                pe.wait_ge(xn1_ready, t + 1)
                for hf in range(2):
                    free(hf)
                    transpose_tiles(xn, hf, x1t_ready)
                    reader[hf] = [(x1t_copied, 2 * t + hf + 1)]

            def queries(t):
                pe.wait_ge(x1t_copied, 2 * (t + 1))
                for hf in range(2):
                    free(hf)
                    project_rows(x1t, WQ, hf, q_ready)
                    reader[hf] = [(q_squared, 2 * t + hf + 1)]

            def q_transposed(t):
                for hf in range(2):
                    free(hf)
                    pe.wait_ge(qn_ready, 2 * (t + 1))
                    transpose_tiles(qn, hf, qt_ready)
                    reader[hf] = [(ql_ready, 2 * t + hf + 1)]

            def keys(b):
                pe.wait_ge(cx_in, 16 * (b + 1))
                for ch in range(2):
                    free(ch)
                    for kc in range(KC):
                        last = pe.matmul(ps_w[:, ch, :], cx[:, kc, P * ch:P * ch + P],
                                         w[:, kc, WK:WV + 1, :].rearrange("p a b -> p (a b)"),
                                         start=(kc == 0), stop=(kc == KC - 1))
                    last.then_inc(kp_ready, 1)
                    reader[ch] = [(v_copied, b + 1)]

            def keys_transposed(b):
                pe.wait_ge(ks_ready, b + 1)
                for n in range(6):
                    free(n % 2)
                    if n < 4:
                        for h in range(4):
                            last = pe.transpose(ps_w[0:ROWS, n % 2, P * h:P * h + P],
                                                ks[:, 0, 2 * n + h // 2, h % 2, :], ident)
                    else:
                        for h in range(8):
                            last = pe.matmul(ps_w[0:ROWS, n % 2, SLOT * h:SLOT * h + M1],
                                             ks[0:M1, 1, 4 * (n - 4) + h // 2, h % 2, :],
                                             aux_sb[0:M1, AUX_ID:AUX_ID + M1], start=True, stop=True)
                    last.then_inc(kt_ready, 1)
                    reader[n % 2] = [(kt_copied, 6 * b + n + 1)]

            def score_units(t, b, par, gr, first, last):
                m = GROUPS * t + gr
                for u in range(first, last + 1):
                    if u == 0:
                        wait(pe, ct_copied, m)
                        if gr == 0:
                            pe.wait_ge(stacked, 16 * 12 * (t + 1))
                            if par == 0:
                                pe.wait_ge(kt_copied, 6 * (b + 1))
                            else:
                                pe.wait_ge(keys_odd, 64 * (b + 1))
                    if u >= 2:
                        pe.wait_ge(b_read, UNITS * m + u - 1)
                    j, g = u // 2, 2 * gr + u % 2
                    pe.matmul(ps_b[:, u % 2, 0:2 * M].rearrange("p (a m) -> p a m", a=2),
                              xq[0:ROW_MAX, par, g, P * j:P * j + P], kb[0:ROW_MAX, par, g, :, 0:M],
                              start=True, stop=True).then_inc(b_ready, 1)

            def maxima_transposed(m):
                pe.wait_ge(cs_ready, m + 1)
                for j in range(J):
                    last = pe.transpose(ps_b[0:8, 0, P * j:P * j + P], cs[:, j].rearrange("p g q -> p (g q)"), ident)
                last.then_inc(ct_ready, 1)

            def attend(t, par, first, last):
                for n in range(first, last + 1):
                    gr, k = n // 5, n % 5
                    if k in (0, 2):
                        pe.wait_ge(max_placed[k // 2], 16 * (GROUPS * t + gr + 1))
                    wait(pe, e_ready, EXPS * t + ((-1, 0, -2)[n] if n < 3 else n - 2))
                    if k < 4:
                        h = 4 * gr + k
                        done = pe.matmul(ps_a[:, n % 3, :], kb[0:ROWS, par, h // 2, h % 2, 0:M0],
                                         xq[0:ROWS, par, h // 2, :], start=True, stop=True)
                    else:
                        for g in (2 * gr, 2 * gr + 1):
                            done = pe.matmul(ps_a[:, n % 3, :], kr[0:ROWS, par, g, :], xq[0:ROWS, par, g, :],
                                             start=(g == 2 * gr), stop=(g == 2 * gr + 1))
                    done.then_inc(a_ready, 1)

            def weigh_values(t, par, gr):
                pe.wait_ge(e_ready, EXPS * t + 5 * gr + 5)
                wait(pe, on_ready, GROUPS * t + gr)
                pe.matmul(ps_o[:, :], vr[:, par, gr, :], e[:, (5 * gr + 4) % 10, :], start=True, stop=False,
                          skip_group_check=True)
                for k in range(4):
                    last = pe.matmul(ps_o[SLOT * k:SLOT * k + SLOT, :], vm[:, par, 4 * gr + k, :],
                                     e[:, (5 * gr + k) % 10, :], start=False, stop=True,
                                     skip_group_check=True)
                last.then_inc(o_ready, 1)

            def values_transposed(t, gr):
                pe.wait_ge(o_copied, GROUPS * t + gr + 1)
                for j in range(J):
                    last = pe.transpose(ps_o[:, P * j:P * j + P], osb[:, P * j:P * j + P], ident)
                last.then_inc(on_t_ready, 1)

            def o_transposed(t):
                pe.wait_ge(on_ready, GROUPS * (t + 1))
                for hf in range(2):
                    transpose_tiles(on, hf, ot_ready)
                    reader[hf] = [(ot_copied, 2 * t + hf + 1)]

            def out_projection(t, hf):
                pe.wait_ge(ot_copied, 2 * (t + 1))
                project_rows(ot, WP, hf, y_ready)
                reader[hf] = [(x2_ready, 2 * t + hf + 1)]

            def x2_transposed(t):
                for hf in range(2):
                    free(hf)
                    pe.wait_ge(xn2_ready, t + 1)
                    transpose_tiles(xn, hf, x2t_ready)
                    reader[hf] = [(x2t_copied, 2 * t + hf + 1)]

            def ffn_keys(t):
                for hf in range(2):
                    free(hf)
                    pe.wait_ge(xk_ready, 2 * (t + 1))
                    for kc in range(KC):
                        last = pe.matmul(ps_w[:, hf, :], w[:, kc, FK, P * hf:P * hf + P], xk[:, kc, :],
                                         start=(kc == 0), stop=(kc == KC - 1))
                    last.then_inc(k2_ready, 1)
                    reader[hf] = [(relu_ready, 2 * t + hf + 1)]

            def ffn_gate(t, hf):
                free(hf)
                pe.wait_ge(xr_ready, 2 * (t + 1))
                project_rows(xr, FR, hf, r_ready)
                reader[hf] = [(tanh_ready, 2 * t + hf + 1)]

            def ffn_values(t, hf):
                free(hf)
                pe.wait_ge(kact_ready, 2 * (t + 1))
                project_rows(xd, FV, hf, kv2_ready)
                reader[hf] = [(gated, 2 * t + hf + 1)]

            def one_round(t, b, par, finish, prepare):
                attend(t, par, 0, 2)
                score_units(t, b, par, 1, 0, 1)
                attend(t, par, 3, 3)
                if finish:
                    o_transposed(t - 1)
                score_units(t, b, par, 1, 2, 3)
                attend(t, par, 4, 4)
                if finish:
                    out_projection(t - 1, 0)
                score_units(t, b, par, 1, 4, 5)
                weigh_values(t, par, 0)
                if finish:
                    out_projection(t - 1, 1)
                score_units(t, b, par, 1, 6, 7)
                if prepare:
                    x1_transposed(t + 1)
                maxima_transposed(GROUPS * t + 1)
                values_transposed(t, 0)
                if prepare:
                    if par == 1:
                        keys(b)
                    queries(t + 1)
                attend(t, par, 5, 7)
                score_units(t, b, par, 2, 0, 1)
                attend(t, par, 8, 8)
                score_units(t, b, par, 2, 2, 3)
                attend(t, par, 9, 9)
                score_units(t, b, par, 2, 4, 5)
                weigh_values(t, par, 1)
                if finish:
                    x2_transposed(t - 1)
                score_units(t, b, par, 2, 6, 7)
                maxima_transposed(GROUPS * t + 2)
                values_transposed(t, 1)
                if prepare:
                    q_transposed(t + 1)
                attend(t, par, 10, 12)
                score_units(t, b, par, 3, 0, 1)
                attend(t, par, 13, 13)
                if finish:
                    ffn_keys(t - 1)
                score_units(t, b, par, 3, 2, 3)
                attend(t, par, 14, 14)
                score_units(t, b, par, 3, 4, 5)
                weigh_values(t, par, 2)
                score_units(t, b, par, 3, 6, 7)
                if prepare and par == 1:
                    keys_transposed(b)
                if finish:
                    ffn_gate(t - 1, 0)
                maxima_transposed(GROUPS * t + 3)
                values_transposed(t, 2)
                if finish:
                    ffn_gate(t - 1, 1)
                attend(t, par, 15, 17)
                if prepare:
                    score_units(t + 1, b, 1 - par, 0, 0, 1)
                attend(t, par, 18, 18)
                if prepare:
                    score_units(t + 1, b, 1 - par, 0, 2, 3)
                attend(t, par, 19, 19)
                if prepare:
                    score_units(t + 1, b, 1 - par, 0, 4, 5)
                if finish:
                    ffn_values(t - 1, 0)
                if prepare:
                    score_units(t + 1, b, 1 - par, 0, 6, 7)
                weigh_values(t, par, 3)
                if prepare:
                    maxima_transposed(GROUPS * (t + 1))
                if finish:
                    ffn_values(t - 1, 1)
                values_transposed(t, 3)

            pe.wait_ge(aux_in, 16)
            x1_transposed(0)
            pe.wait_ge(centred, 1)
            queries(0)
            pe.wait_ge(centred, 2)
            keys(0)
            q_transposed(0)
            keys_transposed(0)
            score_units(0, 0, 0, 0, 0, UNITS - 1)
            maxima_transposed(0)
            pe.wait_ge(w_rest_in, 16)
            rounds(pe, one_round)
            last = BLOCKS - 1
            o_transposed(last)
            for hf in range(2):
                free(hf)
                out_projection(last, hf)
            x2_transposed(last)
            ffn_keys(last)
            for hf in range(2):
                ffn_gate(last, hf)
            for hf in range(2):
                ffn_values(last, hf)

        @block.scalar
        def _(act):
            def normalize_rows(which, t, src, ready, done):
                act.wait_ge(ready, t + 1)
                for j in range(J):
                    last = nc.scalar.activation(xn[:, j, :], src[:, j, :], ACT.Identity,
                                                scale=rs[:, which, j:j + 1], bias=nb[:, which, j:j + 1])
                last.then_inc(done, 1)

            def norm1(t, par):
                normalize_rows(0, t, x_in[:, par], rs1_ready, xn1_ready)

            def norm2(t):
                normalize_rows(1, t, x2, rs2_ready, xn2_ready)

            def x1_copy(t):
                for hf in range(2):
                    act.wait_ge(x1t_ready, 2 * t + hf + 1)
                    nc.scalar.activation(x1t[:, hf, :], ps_w[:, hf, :], ACT.Copy).then_inc(x1t_copied, 1)

            def q_copy(t):
                for hf in range(2):
                    act.wait_ge(q_ready, 2 * t + hf + 1)
                    nc.scalar.activation(qn[:, 2 * hf:2 * hf + 2, :].rearrange("p j c -> p (j c)"),
                                         ps_w[:, hf, :], ACT.Copy)
                    nc.scalar.activation(ql[:, hf, :], ps_w[:, hf, :], ACT.Square).then_inc(q_squared, 1)

            def q_high(t):
                for hf in range(2):
                    act.wait_ge(qt_ready, 2 * t + hf + 1)
                    nc.scalar.activation(qh[:, hf, :].bitcast(F32R), ps_w[:, hf, :],
                                         ACT.Copy).then_inc(qh_ready, 1)

            def keys_copy(b):
                act.wait_ge(kp_ready, 2 * (b + 1))
                nc.scalar.activation(kf[:, :, :], ps_w[:, :, 0:C], ACT.Copy)
                nc.scalar.activation(kt[:, :, :], ps_w[:, :, 0:C], ACT.Square).then_inc(kf_copied, 1)

            def keys_stacked(b):
                wait(act, keys_odd, 64 * b)
                wait(act, a_ready, EXPS * (2 * b - 1))
                for n in range(4):
                    act.wait_ge(kt_ready, 6 * b + n + 1)
                    g = 2 * n
                    nc.scalar.activation(kb[0:ROWS, 0, g:g + 2, :, 0:M0].rearrange("p g j m -> p (g j) m"),
                                         ps_w[0:ROWS, n % 2, :].rearrange("p (h m) -> p h m", m=P),
                                         ACT.Copy).then_inc(kt_copied, 1)
                for n in range(4, 6):
                    act.wait_ge(kt_ready, 6 * b + n + 1)
                    g = 4 * (n - 4)
                    rest = ps_w[0:ROWS, n % 2, 0:8 * SLOT].rearrange("p (g j m) -> p g j m", g=4, j=2)
                    nc.scalar.activation(kb[0:ROWS, 0, g:g + 4, :, M0:M].rearrange("p g j m -> p (g j) m"),
                                         ps_w[0:ROWS, n % 2, 0:8 * SLOT].rearrange("p (h m) -> p h m", m=SLOT)[:, :, 0:M1],
                                         ACT.Copy)
                    for odd in range(2):
                        slots = kr[0:ROWS, 0, g + odd:g + 4:2, 2 * SLOT * odd:2 * SLOT * odd + 2 * SLOT]
                        last = nc.scalar.activation(slots.rearrange("p g (j m) -> p g j m", j=2)[:, :, :, 0:M1],
                                                    rest[:, odd:4:2, :, 0:M1], ACT.Copy)
                    last.then_inc(kt_copied, 1)

            def maxima_copy(m):
                for placed in max_placed:
                    wait(act, placed, 16 * m)
                act.wait_ge(ct_ready, m + 1)
                nc.scalar.activation(ct[:, :], ps_b[0:8, 0, :], ACT.Copy).then_inc(ct_copied, 1)

            def exponentials(t, first, last):
                for n in range(first, last + 1):
                    if n % 5 == 0:
                        wait(act, o_ready, GROUPS * t + n // 5 - 1)
                    act.wait_ge(a_ready, EXPS * t + n + 1)
                    nc.scalar.activation(e[:, n % 10, :], ps_a[:, n % 3, :], ACT.Exp).then_inc(e_ready, 1)

            def o_copy(t, gr):
                act.wait_ge(o_ready, GROUPS * t + gr + 1)
                nc.scalar.activation(osb[:, :], ps_o[:, :], ACT.Copy).then_inc(o_copied, 1)

            def on_copy(t):
                for hf in range(2):
                    act.wait_ge(ot_ready, 2 * t + hf + 1)
                    nc.scalar.activation(ot[:, hf, :], ps_w[:, hf, :], ACT.Copy).then_inc(ot_copied, 1)

            def x2_copy(t, par):
                for hf in range(2):
                    act.wait_ge(x2t_ready, 2 * t + hf + 1)
                    if par == 0:
                        nc.scalar.activation(x2t[:, 1, hf, 0:1], ps_w[:, hf, T - 1:T], ACT.Copy)
                    nc.scalar.activation(x2t[:, par, hf, 1:T + 1], ps_w[:, hf, :],
                                         ACT.Copy).then_inc(x2t_copied, 1)

            def scale_before(t, par, mixed, begun):
                first = KC if mixed is xr else 0
                act.wait_ge(x2t_copied, 2 * (t + 1))
                for hf in range(2):
                    nc.scalar.activation(mixed[:, hf, :], x2t[:, par, hf, 0:T], ACT.Copy,
                                         scale=rest[:, first + hf:first + hf + 1]).then_inc(begun, 1)

            def ffn_activation(t):
                for hf in range(2):
                    act.wait_ge(k2_ready, 2 * t + hf + 1)
                    nc.scalar.activation(xd[:, hf, :], ps_w[:, hf, :], ACT.Relu).then_inc(relu_ready, 1)
                for hf in range(2):
                    act.wait_ge(relu_ready, 2 * t + hf + 1)
                    nc.scalar.activation(xd[:, hf, :], xd[:, hf, :], ACT.Square).then_inc(kact_ready, 1)

            def ffn_tanh(t, hf):
                if hf == 0:
                    wait(act, stored, 16 * (t + 1))
                act.wait_ge(r_ready, 2 * t + hf + 1)
                nc.scalar.activation(rt[:, 2 * hf:2 * hf + 2, :].rearrange("p j c -> p (j c)"),
                                     ps_w[:, hf, :], ACT.Tanh, scale=0.5).then_inc(tanh_ready, 1)

            def ffn_gate(t):
                act.wait_ge(tanh_ready, 2 * (t + 1))
                gate = rt[:, :, :].rearrange("p j c -> p (j c)")
                nc.scalar.activation(gate, gate, ACT.Copy, scale=0.5, bias=0.5).then_inc(gate_ready, 1)

            def one_round(t, b, par, finish, prepare):
                exponentials(t, 0, 3)
                if finish:
                    on_copy(t - 1)
                exponentials(t, 4, 4)
                if prepare:
                    norm1(t + 1, 1 - par)
                o_copy(t, 0)
                if prepare:
                    x1_copy(t + 1)
                maxima_copy(GROUPS * t + 1)
                if prepare:
                    if par == 1:
                        keys_copy(b)
                    q_copy(t + 1)
                exponentials(t, 5, 7)
                exponentials(t, 8, 9)
                if finish:
                    norm2(t - 1)
                o_copy(t, 1)
                if finish:
                    x2_copy(t - 1, 1 - par)
                    scale_before(t - 1, 1 - par, xk, xk_begun)
                maxima_copy(GROUPS * t + 2)
                if prepare:
                    q_high(t + 1)
                exponentials(t, 10, 12)
                if finish:
                    scale_before(t - 1, 1 - par, xr, xr_begun)
                exponentials(t, 13, 13)
                if finish:
                    ffn_activation(t - 1)
                exponentials(t, 14, 14)
                o_copy(t, 2)
                if prepare and par == 1:
                    keys_stacked(b)
                if finish:
                    ffn_tanh(t - 1, 0)
                maxima_copy(GROUPS * t + 3)
                if finish:
                    ffn_tanh(t - 1, 1)
                exponentials(t, 15, 17)
                exponentials(t, 18, 19)
                if finish:
                    ffn_gate(t - 1)
                o_copy(t, 3)
                if prepare:
                    maxima_copy(GROUPS * (t + 1))

            act.dma_start(w[:, :, WQ, :], weights[:, :, WQ, :]).then_inc(wq_in, 16)
            act.dma_start(w[:, :, WK:WV + 1, :], weights[:, :, WK:WV + 1, :]).then_inc(wkv_in, 16)
            act.dma_start(w[:, :, WV + 1:NW, :], weights[:, :, WV + 1:NW, :]).then_inc(w_rest_in, 16)
            norm1(0, 0)
            x1_copy(0)
            q_copy(0)
            keys_copy(0)
            q_high(0)
            keys_stacked(0)
            maxima_copy(0)
            rounds(act, one_round)
            last = BLOCKS - 1
            on_copy(last)
            norm2(last)
            x2_copy(last, 1)
            scale_before(last, 1, xk, xk_begun)
            scale_before(last, 1, xr, xr_begun)
            ffn_activation(last)
            for hf in range(2):
                ffn_tanh(last, hf)
            ffn_gate(last)

        @block.vector
        def _(dve):
            Q_STEPS, K_STEPS = 12, 7
            QH, KH = J * H, 2 * H

            def heads(ap):
                return ap.rearrange("p (h d) -> p h d", d=D)

            def spread(ap, n):
                return ap.unsqueeze(2).broadcast_to([P, n, D])

            def newton(steps, n, times):
                h, y, a = (qst[:, s, 0:n] for s in (1, 2, 3))
                for _ in range(times):
                    steps.then(dve.tensor_tensor(a, y, y, ALU.mult))
                    steps.then(dve.tensor_tensor(a, a, h, ALU.mult))
                    steps.then(dve.scalar_tensor_tensor(y, a, 1.5, y, ALU.add, ALU.mult))

            def row_statistics(which, t, src, done):
                steps = Steps(dve, (ln1_steps, ln2_steps)[which], t)
                for j in range(J):
                    last = dve.bn_stats(st[:, which, j, :], src[:, j, :])
                steps.then(last)
                dve.memset(spare[:, :], 0.0)
                for j in range(J):
                    last = dve.bn_aggr(mv[:, which, j, :], st[:, which, j, :])
                last.then_inc(done, 1)

            def norm1_statistics(t, par):
                dve.wait_ge(x_landed, 16 * (t + 1))
                row_statistics(0, t, x_in[:, par], mv1_ready)

            def norm2_statistics(t):
                dve.wait_ge(x2_ready, 2 * (t + 1))
                row_statistics(1, t, x2, mv2_ready)

            def head_variances(t, b, with_keys):
                steps = Steps(dve, q_steps, Q_STEPS * t)
                if with_keys:
                    dve.wait_ge(kf_copied, b + 1)
                    dve.tensor_reduce(qst[:, 4, QH:QH + KH], kt[:, :, :].rearrange("p a (h d) -> p (a h) d", d=D),
                                      AX_X, ALU.add)
                dve.wait_ge(q_squared, 2 * (t + 1))
                steps.then(dve.tensor_reduce(qst[:, 4, 0:QH], ql[:, :, :].rearrange("p a (h d) -> p (a h) d", d=D),
                                             AX_X, ALU.add))
                n = QH + KH if with_keys else QH
                v, h, y, squares = (qst[:, s, 0:n] for s in (0, 1, 2, 4))
                steps.then(dve.tensor_scalar(v, squares, 1.0 / D, EPS, ALU.mult, ALU.add))
                dve.tensor_scalar(h, v, -0.5, None, ALU.mult)
                steps.then(dve.tensor_scalar(y.bitcast(I32), v.bitcast(I32), -0.5, float(0x5F3759DF),
                                             ALU.mult, ALU.add))
                return steps, n

            def queries(t):
                for hf in range(2):
                    half = heads(qn[:, 2 * hf:2 * hf + 2, :].rearrange("p j c -> p (j c)"))
                    dve.tensor_tensor(half, half, spread(qst[:, 2, 2 * H * hf:2 * H * hf + 2 * H], 2 * H),
                                      ALU.mult).then_inc(qn_ready, 1)

            def q_low(t):
                for hf in range(2):
                    dve.wait_ge(qh_ready, 2 * t + hf + 1)
                    dve.tensor_tensor(ql[:, hf, :].bitcast(F32R), ps_w[:, hf, :], qh[:, hf, :],
                                      ALU.subtract).then_inc(ql_ready, 1)

            def place_values(b):
                wait(dve, o_ready, GROUPS * (2 * b - 1))
                wait(dve, keys_odd, 64 * b)
                dve.wait_ge(kf_copied, b + 1)
                dve.tensor_copy(vm[:, 0, :, 0:D], heads(ps_w[:, 0, C:2 * C]))
                for k in range(4):
                    last = dve.tensor_copy(
                        vr[SLOT * k:SLOT * k + M1, 0, :, SLOT * k:SLOT * k + D],
                        ps_w[0:M1, 1, C:2 * C].rearrange("p (a k d) -> p a k d", k=4, d=D)[:, :, k, :])
                last.then_inc(v_copied, 1)

            kh, kth = (t_[:, :, :].rearrange("p a (h d) -> p (a h) d", d=D) for t_ in (kf, kt))

            def scale_keys(b):
                steps = Steps(dve, k_steps, K_STEPS * b)
                g, bb = (aux_sb[:, a:a + D].unsqueeze(1).broadcast_to([P, 2 * H, D]) for a in (AUX_G, AUX_B))
                gsc, bsc = (gs[:, n, :].unsqueeze(1).broadcast_to([P, 2 * H, D]) for n in range(2))
                steps.then(dve.tensor_tensor(kh, kh, spread(qst[:, 2, QH:QH + KH], 2 * H), ALU.mult))
                steps.then(dve.tensor_tensor(kh, kh, g, ALU.mult))
                steps.then(dve.tensor_tensor(kh, kh, bb, ALU.add))
                steps.then(dve.tensor_tensor(kth, kh, bsc, ALU.mult))
                steps.then(dve.tensor_reduce(kc_sb[:, :], kth, AX_X, ALU.add))
                steps.then(dve.tensor_tensor(kth, kh, gsc, ALU.mult))

            def stack_keys(b):
                steps = Steps(dve, k_steps, K_STEPS * b + K_STEPS - 1)

                def rows(j, first, n):
                    return ks[:, :, :, j, first:first + n].rearrange("p a g n -> p (a g) n")

                def of_head(ap, j):
                    return ap.rearrange("p (g j) n -> p g j n", j=2)[:, :, j, :]

                const = kc_sb[:, :].unsqueeze(2)
                for j in range(2):
                    for row in (ROW_HI, ROW_LO):
                        dve.tensor_copy(rows(j, row + D * j, D).bitcast(F32R), of_head(kth, j))
                    last = dve.tensor_copy(rows(j, ROW_ONE, 1).bitcast(F32R), of_head(const, j))
                steps.then(last)
                for j in range(2):
                    dve.tensor_tensor(rows(j, ROW_HI2 + D * j, D).bitcast(F32R), of_head(kth, j),
                                      rows(j, ROW_HI + D * j, D), ALU.subtract)
                    last = dve.tensor_tensor(rows(j, ROW_ONE + 1, 1).bitcast(F32R), of_head(const, j),
                                             rows(j, ROW_ONE, 1), ALU.subtract)
                last.then_inc(ks_ready, 1)

            def maxima(m, first, last):
                for u in range(first, last + 1):
                    dve.wait_ge(b_ready, UNITS * m + u + 1)
                    dve.tensor_reduce(nmax[:, u // 2, 2 * (u % 2):2 * (u % 2) + 2],
                                      ps_b[:, u % 2, 0:2 * M].rearrange("p (a m) -> p a m", a=2),
                                      AX_X, ALU.max, negate=True).then_inc(b_read, 1)

            def split_maxima(m):
                dve.wait_ge(b_read, UNITS * (m + 1))
                by_head = nmax[:, :, :].rearrange("p j q -> p (j q)")
                high, low = (cs[:, :, :, :].rearrange("p j g (a s) -> p (j g a) s", s=2)[:, :, s] for s in range(2))
                dve.tensor_copy(high.bitcast(F32R), by_head).then_inc(c_steps, 1)
                dve.wait_ge(c_steps, m + 1)
                dve.tensor_tensor(low.bitcast(F32R), by_head, high, ALU.subtract).then_inc(cs_ready, 1)

            def divide(t, gr):
                dve.wait_ge(on_t_ready, GROUPS * t + gr + 1)
                by_slot = ps_o[:, :].rearrange("p (j k d) -> p j k d", k=4, d=SLOT)
                dve.reciprocal(rl[:, :, :], by_slot[:, :, :, D]).then_inc(o_steps, 1)
                dve.wait_ge(o_steps, GROUPS * t + gr + 1)
                dve.tensor_tensor(on[:, :, 4 * D * gr:4 * D * gr + 4 * D].rearrange("p j (k d) -> p j k d", d=D),
                                  by_slot[:, :, :, 0:D], rl[:, :, :].unsqueeze(3).broadcast_to([P, J, 4, D]),
                                  ALU.mult).then_inc(on_ready, 1)

            def residual(t, par, hf):
                if hf == 0:
                    dve.wait_ge(out_ready, 2 * t + 1)
                dve.wait_ge(y_ready, 2 * t + hf + 1)
                dve.tensor_tensor(x2[:, 2 * hf:2 * hf + 2, :].rearrange("p j c -> p (j c)"), ps_w[:, hf, :],
                                  xb[:, par, 2 * hf:2 * hf + 2, :].rearrange("p j c -> p (j c)"),
                                  ALU.add).then_inc(x2_ready, 1)

            def mix(t, par, mixed, begun, done, mu):
                for hf in range(2):
                    dve.wait_ge(begun, 2 * t + hf + 1)
                    dve.scalar_tensor_tensor(mixed[:, hf, :], x2t[:, par, hf, 1:T + 1],
                                             aux_sb[:, mu + hf:mu + hf + 1], mixed[:, hf, :],
                                             ALU.mult, ALU.add).then_inc(done, 1)

            def half_of(ap, hf):
                return ap[:, 2 * hf:2 * hf + 2, :].rearrange("p j c -> p (j c)")

            def gate_values(t):
                dve.wait_ge(gate_ready, t + 1)
                for hf in range(2):
                    dve.wait_ge(kv2_ready, 2 * t + hf + 1)
                    dve.tensor_tensor(half_of(rt, hf), half_of(rt, hf), ps_w[:, hf, :], ALU.mult).then_inc(gated, 1)

            def one_round(t, b, par, finish, prepare):
                new_keys = prepare and par == 1
                m = GROUPS * t + 1
                maxima(m, 0, 1)
                if prepare:
                    norm1_statistics(t + 1, 1 - par)
                maxima(m, 2, 3)
                if finish:
                    residual(t - 1, 1 - par, 0)
                maxima(m, 4, 5)
                if finish:
                    residual(t - 1, 1 - par, 1)
                maxima(m, 6, 7)
                split_maxima(m)
                divide(t, 0)
                if new_keys:
                    place_values(b)
                if finish:
                    norm2_statistics(t - 1)
                maxima(m + 1, 0, 3)
                if prepare:
                    steps, n = head_variances(t + 1, b, new_keys)
                    for u in range(3):
                        newton(steps, n, 1)
                        maxima(m + 1, 4 + u, 4 + u)
                    queries(t + 1)
                else:
                    maxima(m + 1, 4, 6)
                maxima(m + 1, 7, 7)
                split_maxima(m + 1)
                divide(t, 1)
                if finish:
                    mix(t - 1, 1 - par, xk, xk_begun, xk_ready, AUX_MU_K)
                if prepare:
                    q_low(t + 1)
                maxima(m + 2, 0, 1)
                if finish:
                    mix(t - 1, 1 - par, xr, xr_begun, xr_ready, AUX_MU_R)
                if new_keys:
                    scale_keys(b)
                maxima(m + 2, 2, 3)
                if new_keys:
                    stack_keys(b)
                maxima(m + 2, 4, 7)
                split_maxima(m + 2)
                divide(t, 2)
                if prepare:
                    maxima(m + 3, 0, 7)
                    split_maxima(m + 3)
                if finish:
                    gate_values(t - 1)
                divide(t, 3)

            dve.memset(ks[:, :, :, :, :], 0.0).then_inc(w_steps, 1)
            dve.memset(xq[ROW_ONE:ROW_MAX, 0].bitcast(F32), 1.0)
            dve.memset(kb[:, 0].bitcast(F32), 0.0)
            dve.wait_ge(w_steps, 1)
            for j in range(2):
                last = dve.memset(ks[:, :, :, j, ROW_MAX + 2 * j:ROW_MAX + 2 * j + 2], 1.0)
            last.then_inc(w_steps, 1)
            dve.wait_ge(w_steps, 2)
            dve.wait_ge(zeroed, ZEROED)
            norm1_statistics(0, 0)
            for n, (weight, landed) in enumerate(((WQ, wq_in), (WK, wkv_in))):
                dve.wait_ge(landed, 16)
                for kc in range(KC):
                    last = dve.tensor_reduce(wsum[:, n, kc, :], heads(w[:, kc, weight, :]), AX_X, ALU.add)
                last.then_inc(w_steps, 1)
                dve.wait_ge(w_steps, 3 + n)
                for kc in range(KC):
                    last = dve.scalar_tensor_tensor(heads(w[:, kc, weight, :]), spread(wsum[:, n, kc, :], H), -1.0 / D,
                                                    heads(w[:, kc, weight, :]), ALU.mult, ALU.add)
                last.then_inc(centred, 1)
            dve.wait_ge(aux_in, 16)
            dve.tensor_scalar(rest[:, 0:KC], aux_sb[:, AUX_MU_K:AUX_MU_K + KC], -1.0, 1.0, ALU.mult, ALU.add)
            dve.tensor_scalar(rest[:, KC:2 * KC], aux_sb[:, AUX_MU_R:AUX_MU_R + KC], -1.0, 1.0, ALU.mult, ALU.add)
            dve.tensor_scalar(gs[:, 0, :], aux_sb[:, AUX_G:AUX_G + D], SCALE, None, ALU.mult)
            dve.tensor_scalar(gs[:, 1, :], aux_sb[:, AUX_B:AUX_B + D], SCALE, None, ALU.mult).then_inc(w_steps, 1)
            dve.wait_ge(w_steps, 5)
            place_values(0)
            newton(*head_variances(0, 0, True), 3)
            queries(0)
            q_low(0)
            scale_keys(0)
            stack_keys(0)
            maxima(0, 0, UNITS - 1)
            split_maxima(0)
            rounds(dve, one_round)
            last = BLOCKS - 1
            for hf in range(2):
                residual(last, 1, hf)
            norm2_statistics(last)
            mix(last, 1, xk, xk_begun, xk_ready, AUX_MU_K)
            mix(last, 1, xr, xr_begun, xr_ready, AUX_MU_R)
            gate_values(last)

        @block.gpsimd
        def _(pool):
            def rstd(which, t, ready, done, steps_sem):
                pool.wait_ge(ready, t + 1)
                steps = Steps(pool, steps_sem, 2 * t)
                pool.tensor_tensor(nm[:, which, :], mv[:, which, :, 0], minus_one[:, :], ALU.mult)
                steps.then(pool.tensor_tensor(ve[:, which, :], mv[:, which, :, 1], eps[:, :], ALU.add))
                steps.then(pool.tensor_tensor(rs[:, which, :], ve[:, which, :], minus_half[:, :], ALU.pow))
                pool.tensor_tensor(nb[:, which, :], nm[:, which, :], rs[:, which, :], ALU.mult).then_inc(done, 1)

            def with_bias(t, par):
                wait(pool, x2_ready, 2 * (t - 1))
                pool.wait_ge(x_landed, 16 * (t + 1))
                pool.tensor_tensor(xb[:, par], x_in[:, par],
                                   aux_sb[:, AUX_BP:AUX_BP + C].unsqueeze(1).broadcast_to([P, J, C]),
                                   ALU.add).then_inc(xb_ready, 1)

            def output(t):
                for hf in range(2):
                    pool.wait_ge(gated, 2 * t + hf + 1)
                    half = slice(2 * hf, 2 * hf + 2)
                    pool.tensor_tensor(rt[:, half], rt[:, half], x2[:, half], ALU.add).then_inc(out_ready, 1)
                pool.wait_ge(out_ready, 2 * (t + 1) + 1)
                pool.dma_start(out_rows[t], rt[:, :, :]).then_inc(stored, 16)

            def one_round(t, b, par, finish, prepare):
                if prepare:
                    rstd(0, t + 1, mv1_ready, rs1_ready, p1_steps)
                if finish:
                    rstd(1, t - 1, mv2_ready, rs2_ready, p2_steps)
                if prepare:
                    with_bias(t + 1, 1 - par)
                if finish:
                    output(t - 1)

            steps = Steps(pool, zeroed, 0)
            steps.then(pool.memset(cx[:, :, M:2 * P], 0.0))
            steps.then(pool.memset(eps[:, :], EPS))
            steps.then(pool.memset(minus_half[:, :], -0.5))
            steps.then(pool.memset(minus_one[:, :], -1.0))
            steps.then(pool.memset(vm[:, 0], 0.0))
            steps.then(pool.memset(vm[:, 0, :, D:D + 1], 1.0))
            steps.then(pool.memset(vr[:, 0], 0.0))
            for k in range(4):
                steps.then(pool.memset(vr[SLOT * k:SLOT * k + M1, 0, :, SLOT * k + D:SLOT * k + D + 1], 1.0))
            steps.then(pool.memset(kr[:, 0].bitcast(F32), 0.0))
            steps.then(pool.memset(x2t[:, 0, :, 0:1], 0.0))
            steps.then(pool.memset(xq[ROW_ONE:ROW_MAX, 1].bitcast(F32), 1.0))
            assert steps.n == ZEROED
            pool.memset(spare2[:, :], 0.0).then_inc(out_ready, 1)
            pool.wait_ge(out_ready, 1)
            pool.dma_start(spare2[:, :], aux[:, 0:2]).then_inc(stored, 16)
            pool.wait_ge(aux_in, 16)
            rstd(0, 0, mv1_ready, rs1_ready, p1_steps)
            with_bias(0, 0)
            rounds(pool, one_round)
            rstd(1, BLOCKS - 1, mv2_ready, rs2_ready, p2_steps)
            output(BLOCKS - 1)
            pool.wait_ge(stored, 16 * (BLOCKS + 1))


def kernel(x, ctx_1024, L0_xattn_Wq, L0_xattn_Wk, L0_xattn_Wv, L0_xattn_Wp, L0_xattn_bp, L0_xattn_ln_g,
           L0_xattn_ln_b, L0_ffn_W_r, L0_ffn_W_k, L0_ffn_W_v, L0_ffn_mu_r, L0_ffn_mu_k):
    import concourse.bacc as bacc
    from concourse.bass_utils import run_bass_kernel_spmd

    def spread(row):
        return np.broadcast_to(np.asarray(row)[None, :], (P, row.shape[0]))

    def column(vector):
        return np.asarray(vector).reshape(KC, P).T

    stacked = np.stack([np.asarray(m).T for m in (L0_xattn_Wq, L0_xattn_Wk, L0_xattn_Wv, L0_xattn_Wp,
                                                  L0_ffn_W_r, L0_ffn_W_k, L0_ffn_W_v)])
    arrays = {
        "x": np.ascontiguousarray(np.asarray(x).reshape(B * N, C)),
        "context": np.ascontiguousarray(np.asarray(ctx_1024).reshape(B, M, KC, P).transpose(0, 3, 2, 1)),
        "weights": np.ascontiguousarray(stacked.reshape(NW, KC, P, C).transpose(2, 1, 0, 3)),
        "aux": np.ascontiguousarray(np.concatenate(
            [column(L0_ffn_mu_r), column(L0_ffn_mu_k), spread(L0_xattn_ln_g), spread(L0_xattn_ln_b),
             spread(L0_xattn_bp), np.eye(P, dtype=np.float32)], axis=1)),
    }
    nc = bacc.Bacc("TRN2", target_bir_lowering=False, num_devices=1)
    args = [nc.dram_tensor(name, a.shape, mybir.dt.from_np(a.dtype), kind="ExternalInput").ap()
            for name, a in arrays.items()]
    out = nc.dram_tensor("out", (B * N, C), F32, kind="ExternalOutput").ap()
    xattn_ffn(nc, *args, out)
    result = run_bass_kernel_spmd(nc, [arrays], core_ids=[0])
    return result.results[0]["out"].reshape(B, N, C)
```

```python
from contextlib import ExitStack

import numpy as np

import concourse.bass as bass
from concourse import mybir

ALU = mybir.AluOpType
ACT = mybir.ActivationFunctionType
F32 = mybir.dt.float32
F32R = mybir.dt.float32r
I32 = mybir.dt.int32
AX_X = mybir.AxisListType.X

P = 128
B, N, C = 4, 1024, 256
M, H, D = 154, 16, 16
SCALE = 8.0 / D
EPS = 1e-5
T = 512
BLOCKS = B * N // T
J = T // P
KC = C // P
G = H // 2
GROUPS = H // 4
M0, M1 = P, M - P
SLOT = 32
KPAD = M + 6

ROW_HI, ROW_HI2, ROW_LO, ROW_ONE, ROW_MAX, ROWS = 0, 32, 64, 96, 98, 102
WQ, WK, WV, WP, FR, FK, FV = range(7)
NW = 7
AUX_MU_R, AUX_MU_K, AUX_G, AUX_B, AUX_BP, AUX_ID = 0, 2, 4, 20, 36, 36 + C
AUX = AUX_ID + P


def wait(eng, sem, value):
    if isinstance(value, int) and value <= 0:
        return
    eng.wait_ge(sem, value)


class Steps:

    def __init__(self, eng, sem, before):
        self.eng, self.sem, self.before, self.n = eng, sem, before, 0

    def then(self, ins):
        self.n += 1
        ins.then_inc(self.sem, 1)
        self.eng.wait_ge(self.sem, self.before + self.n)


def xattn_ffn(nc, x, context, weights, aux, out):
    x_rows = x.rearrange("(t j p) c -> t p j c", j=J, p=P)
    out_rows = out.rearrange("(t j p) c -> t p j c", j=J, p=P)

    with ExitStack() as stack:
        def sb(name, shape, dt=F32):
            return stack.enter_context(nc.sbuf_tensor(name, shape, dt))

        def ps(name, shape):
            return stack.enter_context(nc.psum_tensor(name, shape, F32))

        def sem(name):
            return stack.enter_context(nc.semaphore(name))

        w = sb("w", [P, KC, NW, C])
        wp_high = sb("wp_high", [P, KC, C], F32R)
        wp_low = sb("wp_low", [P, KC, C], F32R)
        wv_high = sb("wv_high", [P, KC, C], F32R)
        wv_low = sb("wv_low", [P, KC, C], F32R)
        aux_sb = sb("aux_sb", [P, AUX])
        ident = aux_sb[:, AUX_ID:AUX_ID + P]
        minus_half = sb("minus_half", [P, J])
        minus_one = sb("minus_one", [P, J])
        eps = sb("eps", [P, J])
        rest = sb("rest", [P, 2 * KC])
        spare = sb("spare", [P, 2])
        spare2 = sb("spare2", [P, 2])
        gs = sb("gs", [P, 2, D])
        wsum = sb("wsum", [P, 2, KC, H])
        cx = sb("cx", [P, KC, 2 * P])
        kb = sb("kb", [P, 2, G, 2, KPAD], F32R)
        kr = sb("kr", [P, 2, G, P], F32R)
        vm = sb("vm", [P, 2, H, SLOT])
        vr = sb("vr", [P, 2, GROUPS, P])
        ks = sb("ks", [P, G, 2, ROWS])
        ksr = sb("ksr", [P, GROUPS, ROWS])
        kf = sb("kf", [P, 2, C])
        kt = sb("kt", [P, 2, C])
        kc_sb = sb("kc_sb", [P, 2 * H])
        x_in = sb("x_in", [P, 2, J, C])
        st = sb("st", [P, 2, J, 6])
        mv = sb("mv", [P, 2, J, 2])
        ve = sb("ve", [P, 2, J])
        rs = sb("rs", [P, 2, J])
        nm = sb("nm", [P, 2, J])
        nb = sb("nb", [P, 2, J])
        xn = sb("xn", [P, J, C])
        x1t = sb("x1t", [P, KC, T])
        qn = sb("qn", [P, J, C])
        qst = sb("qst", [P, 5, (J + 2) * H])
        qh = sb("qh", [P, KC, T], F32R)
        ql = sb("ql", [P, KC, T])
        xq = sb("xq", [P, 2, G, T], F32R)
        nmax = sb("nmax", [P, J, 4])
        cs = sb("cs", [P, J, 2, 4])
        ct = sb("ct", [8, T])
        e = sb("e", [P, 10, T])
        osb = sb("osb", [P, T])
        rl = sb("rl", [P, J, 4])
        on = sb("on", [P, J, C])
        ot = sb("ot", [P, KC, T], F32R)
        xb = sb("xb", [P, 2, J, C])
        x2 = sb("x2", [P, J, C])
        x2t = sb("x2t", [P, 2, KC, T + 1])
        xd = sb("xd", [P, KC, T])
        xr = sb("xr", [P, KC, T])
        xk = sb("xk", [P, KC, T])
        rt = sb("rt", [P, J, C])

        ps_a = ps("ps_a", [P, 3, T])
        ps_b = ps("ps_b", [P, 2, T])
        ps_o = ps("ps_o", [P, T])
        ps_w = ps("ps_w", [P, 2, T])

        def sems(text):
            return [sem(name) for name in text.split()]

        aux_in, wq_in, wkv_in, w_rest_in, cx_in, zeroed, centred, w_steps = sems(
            "aux_in wq_in wkv_in w_rest_in cx_in zeroed centred w_steps")
        x_landed = sems("x_landed0 x_landed1")
        kp_ready, kf_copied, v_copied, k0_steps, pk_steps, k_products, k_scaled, k_steps, ks_ready = sems(
            "kp_ready kf_copied v_copied k0_steps pk_steps k_products k_scaled k_steps ks_ready")
        kt_ready, kt_copied, keys_odd = sems("kt_ready kt_copied keys_odd")
        mv1_ready, rs1_ready, xn1_ready, x1t_ready, x1t_copied = sems("mv1_ready rs1_ready xn1_ready x1t_ready x1t_copied")
        q_ready, q_squared, q_steps, qn_ready = sems("q_ready q_squared q_steps qn_ready")
        qt_ready, qh_ready, ql_ready, stacked = sems("qt_ready qh_ready ql_ready stacked")
        b_ready, b_read, c_steps, cs_ready, ct_ready, ct_copied = sems(
            "b_ready b_read c_steps cs_ready ct_ready ct_copied")
        max_placed = sems("max_placed0 max_placed1")
        a_ready, e_ready, o_ready, o_copied, on_t_ready, o_steps, on_ready = sems(
            "a_ready e_ready o_ready o_copied on_t_ready o_steps on_ready")
        ot_ready, ot_copied, ot_split, y_ready, xb_ready, x2_ready, w_high, w_split = sems(
            "ot_ready ot_copied ot_split y_ready xb_ready x2_ready w_high w_split")
        mv2_ready, rs2_ready, xn2_ready, x2t_ready, x2t_copied = sems("mv2_ready rs2_ready xn2_ready x2t_ready x2t_copied")
        ln1_steps, ln2_steps, p1_steps, p2_steps, xk_begun, xr_begun, xk_ready, xr_ready = sems(
            "ln1_steps ln2_steps p1_steps p2_steps xk_begun xr_begun xk_ready xr_ready")
        k2_ready, relu_ready, kact_ready, kact_copied, kact_split = sems(
            "k2_ready relu_ready kact_ready kact_copied kact_split")
        r_ready, tanh_ready, gate_ready, kv2_ready, gated, out_ready, stored, xn2_half_ready, last_ready, last_stored = sems(
            "r_ready tanh_ready gate_ready kv2_ready gated out_ready stored xn2_half_ready last_ready last_stored")

        ZEROED = 14
        Q_STEPS = 10
        KP_STEPS = 3
        QH, KH = J * H, 2 * H
        UNITS = 2 * J
        EXPS = 5 * GROUPS

        block = stack.enter_context(nc.Block())

        def rounds(eng, one_round):
            one_round(0, 0, 0, False, True)
            with eng.Fori(0, (BLOCKS - 2) // 2) as i:
                one_round(2 * i + 1, i + 1, 1, True, True)
                one_round(2 * i + 2, i + 1, 0, True, True)
            one_round(BLOCKS - 1, B, 1, True, False)

        @block.sync
        def _(sp):
            def load_x(t, par):
                sp.dma_start(x_in[:, par], x_rows[t]).then_inc(x_landed[par], 16)

            def load_context(b):
                if not (isinstance(b, int) and b == 0):
                    wait(sp, kp_ready, 2 * b)
                sp.dma_start(cx[:, :, 0:M], context[b]).then_inc(cx_in, 16)

            def copy_keys(b):
                wait(sp, o_ready, GROUPS * 2 * b)
                sp.dma_start(kb[0:ROWS, 1].bitcast(F32), kb[0:ROWS, 0].bitcast(F32)).then_inc(keys_odd, 16)
                sp.dma_start(kr[0:ROWS, 1].bitcast(F32), kr[0:ROWS, 0].bitcast(F32)).then_inc(keys_odd, 16)
                sp.dma_start(vm[:, 1], vm[:, 0]).then_inc(keys_odd, 16)
                sp.dma_start(vr[:, 1], vr[:, 0]).then_inc(keys_odd, 16)

            def stack_queries(t, par):
                wait(sp, qh_ready, KC * (t + 1))
                for row, src in ((ROW_HI, qh[:, :, :].bitcast(F32)), (ROW_HI2, qh[:, :, :].bitcast(F32)), (ROW_LO, ql)):
                    if src is ql:
                        wait(sp, ql_ready, KC * (t + 1))
                    for r in range(4):
                        sp.dma_start(xq[row:row + 32, par, r:G:4, :].bitcast(F32),
                                     src[32 * r:32 * r + 32, :, :]).then_inc(stacked, 16)

            def place_maxima(t, par, gr):
                wait(sp, ct_copied, GROUPS * t + gr + 1)
                for g in range(2):
                    sp.dma_start(xq[ROW_MAX:ROWS, par, 2 * gr + g, :].bitcast(F32),
                                 ct[4 * g:4 * g + 4, :]).then_inc(max_placed[g], 16)

            def one_round(t, b, par, finish, prepare):
                if prepare:
                    load_x(t + 2, par)
                    if par == 1:
                        load_context(b)
                if par == 0:
                    copy_keys(b)
                place_maxima(t, par, 1)
                place_maxima(t, par, 2)
                if prepare:
                    stack_queries(t + 1, 1 - par)
                place_maxima(t, par, 3)
                if prepare:
                    place_maxima(t + 1, 1 - par, 0)

            for t in range(2):
                load_x(t, t)
            sp.dma_start(aux_sb[:, :], aux).then_inc(aux_in, 16)
            sp.wait_ge(zeroed, 1)
            load_context(0)
            stack_queries(0, 0)
            place_maxima(0, 0, 0)
            rounds(sp, one_round)
            for hf in range(2):
                sp.wait_ge(last_ready, hf + 1)
                sp.dma_start(out_rows[BLOCKS - 1][:, 2 * hf:2 * hf + 2], rt[:, 2 * hf:2 * hf + 2, :]).then_inc(last_stored, 16)
            sp.wait_ge(last_stored, 32)
            sp.wait_ge(stored, 16 * BLOCKS)

        @block.tensor
        def _(pe):
            reader = [[], []]

            def free(hf):
                for sem_, count in reader[hf]:
                    wait(pe, sem_, count)

            def transpose_tiles(src, hf, done):
                for j in range(J):
                    last = pe.transpose(ps_w[:, hf, P * j:P * j + P], src[:, j, P * hf:P * hf + P], ident)
                last.then_inc(done, 1)

            def project_rows(src, weight, hf, done):
                for j in (2 * hf, 2 * hf + 1):
                    for kc in range(KC):
                        last = pe.matmul(ps_w[:, hf, C * (j % 2):C * (j % 2) + C], src[:, kc, P * j:P * j + P],
                                         w[:, kc, weight, :], start=(kc == 0), stop=(kc == KC - 1))
                last.then_inc(done, 1)

            def project_parts(high, low, w_high, w_low, hf, done):
                for j in (2 * hf, 2 * hf + 1):
                    tile, rows_ = ps_w[:, hf, C * (j % 2):C * (j % 2) + C], slice(P * j, P * j + P)
                    for kc in range(KC):
                        pe.matmul(tile, high[:, kc, rows_], w_high[:, kc, :], start=(kc == 0), stop=False)
                        pe.matmul(tile, high[:, kc, rows_], w_low[:, kc, :], start=False, stop=False)
                        last = pe.matmul(tile, low[:, kc, rows_], w_high[:, kc, :], start=False, stop=(kc == KC - 1))
                last.then_inc(done, 1)

            def x1_transposed(t):
                pe.wait_ge(xn1_ready, t + 1)
                for hf in range(2):
                    free(hf)
                    transpose_tiles(xn, hf, x1t_ready)
                    reader[hf] = [(x1t_copied, 2 * t + hf + 1)]

            def queries(t, hf):
                pe.wait_ge(x1t_copied, 2 * (t + 1))
                free(hf)
                project_rows(x1t, WQ, hf, q_ready)
                reader[hf] = [(q_squared, 2 * t + hf + 1)]

            def q_transposed(t):
                for hf in range(2):
                    free(hf)
                    pe.wait_ge(qn_ready, 2 * (t + 1))
                    transpose_tiles(qn, hf, qt_ready)
                    reader[hf] = [(ql_ready, 2 * t + hf + 1)]

            def keys(b):
                pe.wait_ge(cx_in, 16 * (b + 1))
                for ch in range(2):
                    free(ch)
                    for kc in range(KC):
                        last = pe.matmul(ps_w[:, ch, :], cx[:, kc, P * ch:P * ch + P],
                                         w[:, kc, WK:WV + 1, :].rearrange("p a b -> p (a b)"),
                                         start=(kc == 0), stop=(kc == KC - 1))
                    last.then_inc(kp_ready, 1)
                    reader[ch] = [(v_copied, b + 1)]

            def keys_transposed(b, first, last):
                if first == 0:
                    pe.wait_ge(ks_ready, b + 1)
                for n in range(first, last + 1):
                    free(n % 2)
                    for h in range(4):
                        source = ks[:, 2 * n + h // 2, h % 2, :] if n < 4 else ksr[:, h, :]
                        done = pe.transpose(ps_w[0:ROWS, n % 2, P * h:P * h + P], source, ident)
                    done.then_inc(kt_ready, 1)
                    reader[n % 2] = [(kt_copied, 5 * b + n + 1)]

            def score_units(t, b, par, gr, first, last):
                m = GROUPS * t + gr
                for u in range(first, last + 1):
                    if u == 0:
                        wait(pe, ct_copied, m)
                        if gr == 0:
                            pe.wait_ge(stacked, 16 * 12 * (t + 1))
                            if par == 0:
                                pe.wait_ge(kt_copied, 5 * (b + 1))
                            else:
                                pe.wait_ge(keys_odd, 64 * (b + 1))
                    if u >= 2:
                        pe.wait_ge(b_read, UNITS * m + u - 1)
                    j, g = u // 2, 2 * gr + u % 2
                    pe.matmul(ps_b[:, u % 2, 0:2 * M].rearrange("p (a m) -> p a m", a=2),
                              xq[0:ROW_MAX, par, g, P * j:P * j + P], kb[0:ROW_MAX, par, g, :, 0:M],
                              start=True, stop=True).then_inc(b_ready, 1)

            def maxima_transposed(m):
                pe.wait_ge(cs_ready, m + 1)
                for j in range(J):
                    last = pe.transpose(ps_b[0:8, 0, P * j:P * j + P], cs[:, j].rearrange("p g q -> p (g q)"), ident)
                last.then_inc(ct_ready, 1)

            def attend(t, par, first, last):
                for n in range(first, last + 1):
                    gr, k = n // 5, n % 5
                    if k in (0, 2):
                        pe.wait_ge(max_placed[k // 2], 16 * (GROUPS * t + gr + 1))
                    wait(pe, e_ready, EXPS * t + ((-1, 0, -2)[n] if n < 3 else n - 2))
                    if k < 4:
                        h = 4 * gr + k
                        done = pe.matmul(ps_a[:, n % 3, :], kb[0:ROWS, par, h // 2, h % 2, 0:M0],
                                         xq[0:ROWS, par, h // 2, :], start=True, stop=True)
                    else:
                        for g in (2 * gr, 2 * gr + 1):
                            done = pe.matmul(ps_a[:, n % 3, :], kr[0:ROWS, par, g, :], xq[0:ROWS, par, g, :],
                                             start=(g == 2 * gr), stop=(g == 2 * gr + 1))
                    done.then_inc(a_ready, 1)

            def weigh_values(t, par, gr):
                pe.wait_ge(e_ready, EXPS * t + 5 * gr + 5)
                wait(pe, on_ready, GROUPS * t + gr)
                pe.matmul(ps_o[:, :], vr[:, par, gr, :], e[:, (5 * gr + 4) % 10, :], start=True, stop=False,
                          skip_group_check=True)
                for k in range(4):
                    last = pe.matmul(ps_o[SLOT * k:SLOT * k + SLOT, :], vm[:, par, 4 * gr + k, :],
                                     e[:, (5 * gr + k) % 10, :], start=False, stop=True,
                                     skip_group_check=True)
                last.then_inc(o_ready, 1)

            def values_transposed(t, gr):
                pe.wait_ge(o_copied, GROUPS * t + gr + 1)
                for j in range(J):
                    last = pe.transpose(ps_o[:, P * j:P * j + P], osb[:, P * j:P * j + P], ident)
                last.then_inc(on_t_ready, 1)

            def o_transposed(t):
                pe.wait_ge(on_ready, GROUPS * (t + 1))
                for hf in range(2):
                    pe.wait_ge(gated, 2 * t + hf + 1)
                    transpose_tiles(on, hf, ot_ready)
                    reader[hf] = [(ot_split, 2 * t + hf + 1)]

            def out_projection(t, hf):
                free(hf)
                pe.wait_ge(ot_split, 2 * (t + 1))
                project_parts(ot, qh, wp_high, wp_low, hf, y_ready)
                reader[hf] = [(x2_ready, 2 * t + hf + 1)]

            def x2_transposed(t):
                for hf in range(2):
                    free(hf)
                    pe.wait_ge(xn2_ready, t + 1)
                    transpose_tiles(xn, hf, x2t_ready)
                    reader[hf] = [(x2t_copied, 2 * t + hf + 1)]

            def ffn_keys(t, hf):
                free(hf)
                pe.wait_ge(xk_ready, 2 * (t + 1))
                for kc in range(KC):
                    last = pe.matmul(ps_w[:, hf, :], w[:, kc, FK, P * hf:P * hf + P], xk[:, kc, :],
                                     start=(kc == 0), stop=(kc == KC - 1))
                last.then_inc(k2_ready, 1)
                reader[hf] = [(relu_ready, 2 * t + hf + 1)]

            def ffn_gate(t, hf):
                free(hf)
                pe.wait_ge(xr_ready, 2 * (t + 1))
                project_rows(xr, FR, hf, r_ready)
                reader[hf] = [(tanh_ready, 2 * t + hf + 1)]

            def ffn_values(t, hf):
                free(hf)
                pe.wait_ge(kact_split, t + 1)
                project_parts(ot, qh, wv_high, wv_low, hf, kv2_ready)
                reader[hf] = [(gated, 2 * t + hf + 3)]

            def one_round(t, b, par, finish, prepare):
                score_units(t, b, par, 1, 0, 1)
                if finish:
                    o_transposed(t - 1)
                attend(t, par, 0, 3)
                score_units(t, b, par, 1, 2, 3)
                attend(t, par, 4, 4)
                score_units(t, b, par, 1, 4, 5)
                if prepare and par == 1:
                    keys(b)
                elif finish:
                    out_projection(t - 1, 0)
                weigh_values(t, par, 0)
                score_units(t, b, par, 1, 6, 7)
                if prepare and par == 1:
                    out_projection(t - 1, 0)
                if finish:
                    out_projection(t - 1, 1)
                maxima_transposed(GROUPS * t + 1)
                if prepare:
                    x1_transposed(t + 1)
                values_transposed(t, 0)
                score_units(t, b, par, 2, 0, 1)
                if prepare:
                    queries(t + 1, 0)
                attend(t, par, 5, 7)
                if prepare:
                    queries(t + 1, 1)
                score_units(t, b, par, 2, 2, 3)
                attend(t, par, 8, 9)
                score_units(t, b, par, 2, 4, 7)
                weigh_values(t, par, 1)
                maxima_transposed(GROUPS * t + 2)
                if finish:
                    x2_transposed(t - 1)
                values_transposed(t, 1)
                score_units(t, b, par, 3, 0, 1)
                if prepare:
                    q_transposed(t + 1)
                attend(t, par, 10, 13)
                if finish:
                    ffn_keys(t - 1, 0)
                score_units(t, b, par, 3, 2, 3)
                if finish:
                    ffn_keys(t - 1, 1)
                score_units(t, b, par, 3, 4, 5)
                attend(t, par, 14, 14)
                score_units(t, b, par, 3, 6, 7)
                weigh_values(t, par, 2)
                maxima_transposed(GROUPS * t + 3)
                if finish:
                    ffn_gate(t - 1, 0)
                values_transposed(t, 2)
                if prepare and par == 1:
                    keys_transposed(b, 0, 4)
                if finish:
                    ffn_gate(t - 1, 1)
                if prepare:
                    score_units(t + 1, b, 1 - par, 0, 0, 1)
                attend(t, par, 15, 18)
                if prepare:
                    score_units(t + 1, b, 1 - par, 0, 2, 3)
                attend(t, par, 19, 19)
                if prepare:
                    score_units(t + 1, b, 1 - par, 0, 4, 5)
                if finish:
                    ffn_values(t - 1, 0)
                if prepare:
                    score_units(t + 1, b, 1 - par, 0, 6, 7)
                weigh_values(t, par, 3)
                if prepare:
                    maxima_transposed(GROUPS * (t + 1))
                values_transposed(t, 3)
                if finish:
                    ffn_values(t - 1, 1)

            pe.wait_ge(aux_in, 16)
            x1_transposed(0)
            pe.wait_ge(centred, 1)
            keys(0)
            pe.wait_ge(centred, 2)
            for hf in range(2):
                queries(0, hf)
            q_transposed(0)
            keys_transposed(0, 0, 4)
            score_units(0, 0, 0, 0, 0, UNITS - 1)
            maxima_transposed(0)
            pe.wait_ge(w_split, 2)
            rounds(pe, one_round)
            last = BLOCKS - 1
            o_transposed(last)
            for hf in range(2):
                free(hf)
                out_projection(last, hf)
            pe.wait_ge(xn2_half_ready, 1)
            x2_transposed(last)
            for hf in range(2):
                ffn_keys(last, hf)
            for hf in range(2):
                ffn_gate(last, hf)
            for hf in range(2):
                ffn_values(last, hf)

        @block.scalar
        def _(act):
            def normalize_rows(which, t, src, ready, done, tiles=J):
                act.wait_ge(ready, t + 1)
                for j in range(tiles):
                    last = nc.scalar.activation(xn[:, j, :], src[:, j, :], ACT.Identity,
                                                scale=rs[:, which, j:j + 1], bias=nb[:, which, j:j + 1])
                last.then_inc(done, 1)

            def norm1(t, par):
                normalize_rows(0, t, x_in[:, par], rs1_ready, xn1_ready)

            def norm2(t):
                normalize_rows(1, t, x2, rs2_ready, xn2_ready)

            def x1_copy(t):
                for hf in range(2):
                    act.wait_ge(x1t_ready, 2 * t + hf + 1)
                    nc.scalar.activation(x1t[:, hf, :], ps_w[:, hf, :], ACT.Copy).then_inc(x1t_copied, 1)

            def q_copy(t, hf):
                act.wait_ge(q_ready, 2 * t + hf + 1)
                nc.scalar.activation(qn[:, 2 * hf:2 * hf + 2, :].rearrange("p j c -> p (j c)"),
                                     ps_w[:, hf, :], ACT.Copy)
                nc.scalar.activation(ql[:, hf, :], ps_w[:, hf, :], ACT.Square).then_inc(q_squared, 1)

            def q_high(t):
                for hf in range(2):
                    act.wait_ge(qt_ready, 2 * t + hf + 1)
                    nc.scalar.activation(qh[:, hf, :], ps_w[:, hf, :],
                                         ACT.Copy).then_inc(qh_ready, 1)

            def keys_copy(b):
                act.wait_ge(kp_ready, 2 * (b + 1))
                nc.scalar.activation(kf[:, :, :], ps_w[:, :, 0:C], ACT.Copy)
                nc.scalar.activation(kt[:, :, :], ps_w[:, :, 0:C], ACT.Square).then_inc(kf_copied, 1)

            def keys_stacked(b, first, last):
                if first == 0:
                    wait(act, keys_odd, 64 * b)
                    wait(act, a_ready, EXPS * (2 * b - 1))
                for n in range(first, min(last + 1, 4)):
                    act.wait_ge(kt_ready, 5 * b + n + 1)
                    g = 2 * n
                    nc.scalar.activation(kb[0:ROWS, 0, g:g + 2, :, 0:M0].rearrange("p g j m -> p (g j) m"),
                                         ps_w[0:ROWS, n % 2, :].rearrange("p (h m) -> p h m", m=P),
                                         ACT.Copy).then_inc(kt_copied, 1)
                if last == 4:
                    act.wait_ge(kt_ready, 5 * b + 5)
                    rest_keys = ps_w[0:ROWS, 0, :].rearrange("p (a k m) -> p a k m", k=4, m=SLOT)
                    nc.scalar.activation(kb[0:ROWS, 0, :, :, M0:M].rearrange("p g j m -> p (g j) m"),
                                         ps_w[0:ROWS, 0, :].rearrange("p (h m) -> p h m", m=SLOT)[:, :, 0:M1],
                                         ACT.Copy)
                    for odd in range(2):
                        slots = kr[0:ROWS, 0, odd:G:2, 2 * SLOT * odd:2 * SLOT * odd + 2 * SLOT]
                        done = nc.scalar.activation(slots.rearrange("p a (j m) -> p a j m", j=2)[:, :, :, 0:M1],
                                                    rest_keys[:, :, 2 * odd:2 * odd + 2, 0:M1], ACT.Copy)
                    done.then_inc(kt_copied, 1)

            def maxima_copy(m):
                for placed in max_placed:
                    wait(act, placed, 16 * m)
                act.wait_ge(ct_ready, m + 1)
                nc.scalar.activation(ct[:, :], ps_b[0:8, 0, :], ACT.Copy).then_inc(ct_copied, 1)

            def exponentials(t, first, last):
                for n in range(first, last + 1):
                    if n % 5 == 0:
                        wait(act, o_ready, GROUPS * t + n // 5 - 1)
                    act.wait_ge(a_ready, EXPS * t + n + 1)
                    nc.scalar.activation(e[:, n % 10, :], ps_a[:, n % 3, :], ACT.Exp).then_inc(e_ready, 1)

            def o_copy(t, gr):
                act.wait_ge(o_ready, GROUPS * t + gr + 1)
                nc.scalar.activation(osb[:, :], ps_o[:, :], ACT.Copy).then_inc(o_copied, 1)

            def on_copy(t):
                for hf in range(2):
                    act.wait_ge(ot_ready, 2 * t + hf + 1)
                    nc.scalar.activation(ot[:, hf, :], ps_w[:, hf, :], ACT.Copy).then_inc(ot_copied, 1)

            def x2_copy(t, par):
                for hf in range(2):
                    act.wait_ge(x2t_ready, 2 * t + hf + 1)
                    if par == 0:
                        nc.scalar.activation(x2t[:, 1, hf, 0:1], ps_w[:, hf, T - 1:T], ACT.Copy)
                    nc.scalar.activation(x2t[:, par, hf, 1:T + 1], ps_w[:, hf, :],
                                         ACT.Copy).then_inc(x2t_copied, 1)

            def scale_before(t, par, mixed, begun):
                first = KC if mixed is xr else 0
                act.wait_ge(x2t_copied, 2 * (t + 1))
                for hf in range(2):
                    nc.scalar.activation(mixed[:, hf, :], x2t[:, par, hf, 0:T], ACT.Copy,
                                         scale=rest[:, first + hf:first + hf + 1]).then_inc(begun, 1)

            def ffn_relu(t):
                for hf in range(2):
                    act.wait_ge(k2_ready, 2 * t + hf + 1)
                    nc.scalar.activation(xd[:, hf, :], ps_w[:, hf, :], ACT.Relu).then_inc(relu_ready, 1)

            def ffn_square(t):
                for hf in range(2):
                    act.wait_ge(relu_ready, 2 * t + hf + 1)
                    nc.scalar.activation(xd[:, hf, :], xd[:, hf, :], ACT.Square).then_inc(kact_ready, 1)

            def ffn_tanh(t, hf):
                if hf == 0:
                    wait(act, stored, 16 * (t + 1))
                act.wait_ge(r_ready, 2 * t + hf + 1)
                nc.scalar.activation(rt[:, 2 * hf:2 * hf + 2, :].rearrange("p j c -> p (j c)"),
                                     ps_w[:, hf, :], ACT.Tanh, scale=0.5).then_inc(tanh_ready, 1)

            def kact_high(t):
                act.wait_ge(kact_ready, 2 * (t + 1))
                nc.scalar.activation(ot[:, :, :], xd[:, :, :], ACT.Copy).then_inc(kact_copied, 1)

            def ffn_gate(t):
                act.wait_ge(tanh_ready, 2 * (t + 1))
                gate = rt[:, :, :].rearrange("p j c -> p (j c)")
                nc.scalar.activation(gate, gate, ACT.Copy, scale=0.5, bias=0.5).then_inc(gate_ready, 1)

            def one_round(t, b, par, finish, prepare):
                if finish:
                    on_copy(t - 1)
                exponentials(t, 0, 4)
                if prepare and par == 1:
                    keys_copy(b)
                o_copy(t, 0)
                maxima_copy(GROUPS * t + 1)
                if prepare:
                    x1_copy(t + 1)
                if prepare:
                    q_copy(t + 1, 0)
                exponentials(t, 5, 7)
                if prepare:
                    q_copy(t + 1, 1)
                exponentials(t, 8, 9)
                if finish:
                    norm2(t - 1)
                o_copy(t, 1)
                maxima_copy(GROUPS * t + 2)
                if finish:
                    x2_copy(t - 1, 1 - par)
                    scale_before(t - 1, 1 - par, xk, xk_begun)
                if prepare:
                    q_high(t + 1)
                exponentials(t, 10, 12)
                if finish:
                    scale_before(t - 1, 1 - par, xr, xr_begun)
                exponentials(t, 13, 13)
                if finish:
                    ffn_relu(t - 1)
                exponentials(t, 14, 14)
                if finish:
                    ffn_square(t - 1)
                o_copy(t, 2)
                maxima_copy(GROUPS * t + 3)
                if finish:
                    kact_high(t - 1)
                    ffn_tanh(t - 1, 0)
                if prepare and par == 1:
                    keys_stacked(b, 0, 4)
                if finish:
                    ffn_tanh(t - 1, 1)
                exponentials(t, 15, 17)
                exponentials(t, 18, 19)
                if finish:
                    ffn_gate(t - 1)
                if prepare:
                    norm1(t + 2, par)
                o_copy(t, 3)
                if prepare:
                    maxima_copy(GROUPS * (t + 1))

            act.dma_start(w[:, :, WK:WV + 1, :], weights[:, :, WK:WV + 1, :]).then_inc(wkv_in, 16)
            act.dma_start(w[:, :, WQ, :], weights[:, :, WQ, :]).then_inc(wq_in, 16)
            act.dma_start(w[:, :, WV + 1:NW, :], weights[:, :, WV + 1:NW, :]).then_inc(w_rest_in, 16)
            norm1(0, 0)
            x1_copy(0)
            keys_copy(0)
            for hf in range(2):
                q_copy(0, hf)
            q_high(0)
            act.wait_ge(w_rest_in, 16)
            nc.scalar.activation(wp_high[:, :, :], w[:, :, WP, :], ACT.Copy).then_inc(w_high, 1)
            nc.scalar.activation(wv_high[:, :, :], w[:, :, FV, :], ACT.Copy).then_inc(w_high, 1)
            keys_stacked(0, 0, 4)
            norm1(1, 1)
            maxima_copy(0)
            rounds(act, one_round)
            last = BLOCKS - 1
            on_copy(last)
            normalize_rows(1, last, x2, rs2_ready, xn2_ready, J // 2)
            x2_copy(last, 1)
            scale_before(last, 1, xk, xk_begun)
            scale_before(last, 1, xr, xr_begun)
            ffn_relu(last)
            ffn_square(last)
            kact_high(last)
            for hf in range(2):
                ffn_tanh(last, hf)
            ffn_gate(last)

        @block.vector
        def _(dve):
            K_STEPS = 2

            def heads(ap):
                return ap.rearrange("p (h d) -> p h d", d=D)

            def spread(ap, n):
                return ap.unsqueeze(2).broadcast_to([P, n, D])

            def guess(steps, heads_):
                v, h, y, squares = (qst[:, s, heads_] for s in (0, 1, 2, 4))
                steps.then(dve.tensor_scalar(v, squares, 1.0 / D, EPS, ALU.mult, ALU.add))
                dve.tensor_scalar(h, v, -0.5 * 0.375 ** 3, None, ALU.mult)
                steps.then(dve.tensor_scalar(y.bitcast(I32), v.bitcast(I32), -0.5, float(0x5F3759DF),
                                             ALU.mult, ALU.add))

            def refine(steps, heads_):
                v, y, a = (qst[:, s, heads_] for s in (0, 2, 3))
                steps.then(dve.tensor_tensor(a, y, y, ALU.mult))
                steps.then(dve.tensor_tensor(a, a, v, ALU.mult))
                steps.then(dve.scalar_tensor_tensor(a, a, -10.0 / 3.0, a, ALU.add, ALU.mult))
                steps.then(dve.scalar_tensor_tensor(y, a, 5.0, y, ALU.add, ALU.mult))

            def newton(steps, heads_):
                h, y, a = (qst[:, s, heads_] for s in (1, 2, 3))
                steps.then(dve.tensor_tensor(a, y, y, ALU.mult))
                steps.then(dve.tensor_tensor(a, a, h, ALU.mult))
                steps.then(dve.scalar_tensor_tensor(y, a, 1.5 * 0.375, y, ALU.add, ALU.mult))

            def row_statistics(which, t, src, done):
                steps = Steps(dve, (ln1_steps, ln2_steps)[which], t)
                for j in range(J):
                    last = dve.bn_stats(st[:, which, j, :], src[:, j, :])
                steps.then(last)
                dve.memset(spare[:, :], 0.0)
                for j in range(J):
                    last = dve.bn_aggr(mv[:, which, j, :], st[:, which, j, :])
                last.then_inc(done, 1)

            def norm1_statistics(t, par, loads):
                dve.wait_ge(x_landed[par], 16 * loads)
                row_statistics(0, t, x_in[:, par], mv1_ready)

            def norm2_statistics(t):
                dve.wait_ge(x2_ready, 2 * (t + 1))
                row_statistics(1, t, x2, mv2_ready)

            def square_sums_q(t, hf):
                dve.wait_ge(q_squared, 2 * t + hf + 1)
                return dve.tensor_reduce(qst[:, 4, 2 * H * hf:2 * H * hf + 2 * H], heads(ql[:, hf, :]), AX_X, ALU.add)

            def square_sums_k(b):
                dve.wait_ge(kf_copied, b + 1)
                return dve.tensor_reduce(qst[:, 4, QH:QH + KH], kt[:, :, :].rearrange("p a (h d) -> p (a h) d", d=D),
                                         AX_X, ALU.add)

            def queries(t):
                for hf in range(2):
                    half = heads(qn[:, 2 * hf:2 * hf + 2, :].rearrange("p j c -> p (j c)"))
                    dve.tensor_tensor(half, half, spread(qst[:, 2, 2 * H * hf:2 * H * hf + 2 * H], 2 * H),
                                      ALU.mult).then_inc(qn_ready, 1)

            def q_low(t):
                for hf in range(2):
                    dve.wait_ge(qh_ready, 2 * t + hf + 1)
                    dve.tensor_tensor(ql[:, hf, :].bitcast(F32R), ps_w[:, hf, :], qh[:, hf, :].bitcast(F32),
                                      ALU.subtract).then_inc(ql_ready, 1)

            def place_values(b):
                wait(dve, o_ready, GROUPS * (2 * b - 1))
                wait(dve, keys_odd, 64 * b)
                dve.wait_ge(kf_copied, b + 1)
                dve.tensor_copy(vm[:, 0, :, 0:D], heads(ps_w[:, 0, C:2 * C]))
                for k in range(4):
                    last = dve.tensor_copy(
                        vr[SLOT * k:SLOT * k + M1, 0, :, SLOT * k:SLOT * k + D],
                        ps_w[0:M1, 1, C:2 * C].rearrange("p (a k d) -> p a k d", k=4, d=D)[:, :, k, :])
                last.then_inc(v_copied, 1)

            kh, kth = (t_[:, :, :].rearrange("p a (h d) -> p (a h) d", d=D) for t_ in (kf, kt))

            def stack_keys(b):
                steps = Steps(dve, k_steps, K_STEPS * b)
                dve.wait_ge(k_products, b + 1)
                steps.then(dve.tensor_reduce(kc_sb[:, :], kth, AX_X, ALU.add))
                dve.wait_ge(k_scaled, b + 1)
                const = kc_sb[:, :].unsqueeze(2)

                parts = []
                for j in range(2):
                    parts.append((j, ks[:, :, j, :], *(ap[:, 0:H].rearrange("p (g j) n -> p g j n", j=2)[:, :, j, :]
                                                       for ap in (kh, const))))
                for k in range(4):
                    parts.append((k % 2, ksr[SLOT * k:SLOT * k + M1], *(
                        ap[0:M1, H:2 * H].rearrange("p (a k) n -> p a k n", k=4)[:, :, k, :] for ap in (kh, const))))
                for j, place, key, const_ in parts:
                    for row in (ROW_HI + D * j, ROW_LO + D * j):
                        dve.tensor_copy(place[:, :, row:row + D].bitcast(F32R), key)
                    last = dve.tensor_copy(place[:, :, ROW_ONE:ROW_ONE + 1].bitcast(F32R), const_)
                steps.then(last)
                for j, place, key, const_ in parts:
                    high, low = ROW_HI + D * j, ROW_HI2 + D * j
                    dve.tensor_tensor(place[:, :, low:low + D].bitcast(F32R), key, place[:, :, high:high + D],
                                      ALU.subtract)
                    last = dve.tensor_tensor(place[:, :, ROW_ONE + 1:ROW_ONE + 2].bitcast(F32R), const_,
                                             place[:, :, ROW_ONE:ROW_ONE + 1], ALU.subtract)
                last.then_inc(ks_ready, 1)

            def maxima(m, first, last):
                for u in range(first, last + 1):
                    dve.wait_ge(b_ready, UNITS * m + u + 1)
                    dve.tensor_reduce(nmax[:, u // 2, 2 * (u % 2):2 * (u % 2) + 2],
                                      ps_b[:, u % 2, 0:2 * M].rearrange("p (a m) -> p a m", a=2),
                                      AX_X, ALU.max, negate=True).then_inc(b_read, 1)

            def split_maxima(m):
                dve.wait_ge(b_read, UNITS * (m + 1))
                by_head = nmax[:, :, :].rearrange("p j q -> p (j q)")
                high, low = (cs[:, :, :, :].rearrange("p j g (a s) -> p (j g a) s", s=2)[:, :, s] for s in range(2))
                dve.tensor_copy(high.bitcast(F32R), by_head).then_inc(c_steps, 1)
                dve.wait_ge(c_steps, m + 1)
                dve.tensor_tensor(low.bitcast(F32R), by_head, high, ALU.subtract).then_inc(cs_ready, 1)

            def divide(t, gr):
                dve.wait_ge(on_t_ready, GROUPS * t + gr + 1)
                by_slot = ps_o[:, :].rearrange("p (j k d) -> p j k d", k=4, d=SLOT)
                dve.reciprocal(rl[:, :, :], by_slot[:, :, :, D]).then_inc(o_steps, 1)
                dve.wait_ge(o_steps, GROUPS * t + gr + 1)
                dve.tensor_tensor(on[:, :, 4 * D * gr:4 * D * gr + 4 * D].rearrange("p j (k d) -> p j k d", d=D),
                                  by_slot[:, :, :, 0:D], rl[:, :, :].unsqueeze(3).broadcast_to([P, J, 4, D]),
                                  ALU.mult).then_inc(on_ready, 1)

            def ot_low(t):
                for hf in range(2):
                    dve.wait_ge(ot_copied, 2 * t + hf + 1)
                    dve.tensor_tensor(qh[:, hf, :], ps_w[:, hf, :], ot[:, hf, :].bitcast(F32),
                                      ALU.subtract).then_inc(ot_split, 1)

            def residual(t, par, hf):
                if hf == 0:
                    dve.wait_ge(out_ready, 2 * t + 1)
                dve.wait_ge(y_ready, 2 * t + hf + 1)
                dve.tensor_tensor(x2[:, 2 * hf:2 * hf + 2, :].rearrange("p j c -> p (j c)"), ps_w[:, hf, :],
                                  xb[:, par, 2 * hf:2 * hf + 2, :].rearrange("p j c -> p (j c)"),
                                  ALU.add).then_inc(x2_ready, 1)

            def mix(t, par, mixed, begun, done, mu):
                for hf in range(2):
                    dve.wait_ge(begun, 2 * t + hf + 1)
                    dve.scalar_tensor_tensor(mixed[:, hf, :], x2t[:, par, hf, 1:T + 1],
                                             aux_sb[:, mu + hf:mu + hf + 1], mixed[:, hf, :],
                                             ALU.mult, ALU.add).then_inc(done, 1)

            def half_of(ap, hf):
                return ap[:, 2 * hf:2 * hf + 2, :].rearrange("p j c -> p (j c)")

            def gate_values(t, hf):
                dve.wait_ge(gate_ready, t + 1)
                dve.wait_ge(kv2_ready, 2 * t + hf + 1)
                dve.tensor_tensor(half_of(rt, hf), half_of(rt, hf), ps_w[:, hf, :], ALU.mult).then_inc(gated, 1)

            def one_round(t, b, par, finish, prepare):
                new_keys = prepare and par == 1
                m = GROUPS * t + 1
                maxima(m, 0, 1)
                if finish:
                    ot_low(t - 1)
                maxima(m, 2, 5)
                if new_keys:
                    place_values(b)
                if finish and not new_keys:
                    residual(t - 1, 1 - par, 0)
                maxima(m, 6, 7)
                split_maxima(m)
                if new_keys:
                    residual(t - 1, 1 - par, 0)
                if finish:
                    residual(t - 1, 1 - par, 1)
                divide(t, 0)
                if finish:
                    norm2_statistics(t - 1)
                maxima(m + 1, 0, 1)
                if prepare:
                    steps = Steps(dve, q_steps, Q_STEPS * (t + 1))
                    if new_keys:
                        square_sums_k(b)
                    square_sums_q(t + 1, 0)
                    maxima(m + 1, 2, 3)
                    steps.then(square_sums_q(t + 1, 1))
                    heads_ = slice(0, QH + KH if new_keys else QH)
                    maxima(m + 1, 4, 5)
                    guess(steps, heads_)
                    maxima(m + 1, 6, 7)
                else:
                    maxima(m + 1, 2, 7)
                split_maxima(m + 1)
                if prepare:
                    refine(steps, heads_)
                    newton(steps, heads_)
                    queries(t + 1)
                divide(t, 1)
                if finish:
                    mix(t - 1, 1 - par, xk, xk_begun, xk_ready, AUX_MU_K)
                if prepare:
                    q_low(t + 1)
                maxima(m + 2, 0, 1)
                if finish:
                    mix(t - 1, 1 - par, xr, xr_begun, xr_ready, AUX_MU_R)
                maxima(m + 2, 2, 7)
                split_maxima(m + 2)
                if new_keys:
                    stack_keys(b)
                divide(t, 2)
                if prepare:
                    norm1_statistics(t + 2, par, b + 1 + (par == 0))
                if prepare:
                    maxima(m + 3, 0, 7)
                    split_maxima(m + 3)
                if finish:
                    gate_values(t - 1, 0)
                divide(t, 3)
                if finish:
                    gate_values(t - 1, 1)

            dve.memset(spare[:, :], 0.0).then_inc(gated, 2)
            norm1_statistics(0, 0, 1)
            for n, (weight, landed) in enumerate(((WK, wkv_in), (WQ, wq_in))):
                dve.wait_ge(landed, 16)
                for kc in range(KC):
                    last = dve.tensor_reduce(wsum[:, n, kc, :], heads(w[:, kc, weight, :]), AX_X, ALU.add)
                last.then_inc(w_steps, 1)
                dve.wait_ge(w_steps, 1 + n)
                for kc in range(KC):
                    last = dve.scalar_tensor_tensor(heads(w[:, kc, weight, :]), spread(wsum[:, n, kc, :], H), -1.0 / D,
                                                    heads(w[:, kc, weight, :]), ALU.mult, ALU.add)
                last.then_inc(centred, 1)
            dve.wait_ge(aux_in, 16)
            dve.tensor_scalar(rest[:, 0:KC], aux_sb[:, AUX_MU_K:AUX_MU_K + KC], -1.0, 1.0, ALU.mult, ALU.add)
            dve.tensor_scalar(rest[:, KC:2 * KC], aux_sb[:, AUX_MU_R:AUX_MU_R + KC], -1.0, 1.0, ALU.mult, ALU.add)
            dve.tensor_scalar(gs[:, 0, :], aux_sb[:, AUX_G:AUX_G + D], SCALE, None, ALU.mult)
            dve.tensor_scalar(gs[:, 1, :], aux_sb[:, AUX_B:AUX_B + D], SCALE, None, ALU.mult).then_inc(w_steps, 1)
            dve.memset(ks[:, :, :, :], 0.0)
            dve.memset(ksr[:, :, :], 0.0).then_inc(w_steps, 1)
            dve.memset(xq[ROW_ONE:ROW_MAX, 0].bitcast(F32), 1.0)
            dve.wait_ge(zeroed, ZEROED)
            place_values(0)
            steps = Steps(dve, k0_steps, 0)
            steps.then(square_sums_k(0))
            heads_ = slice(QH, QH + KH)
            guess(steps, heads_)
            refine(steps, heads_)
            newton(steps, heads_)
            assert steps.n == Q_STEPS
            dve.wait_ge(w_steps, 4)
            for j in range(2):
                dve.memset(ks[:, :, j, ROW_MAX + 2 * j:ROW_MAX + 2 * j + 2], 1.0)
            for k in range(4):
                row = ROW_MAX + 2 * (k % 2)
                last = dve.memset(ksr[SLOT * k:SLOT * k + SLOT, :, row:row + 2], 1.0)
            last.then_inc(w_steps, 1)
            dve.wait_ge(w_steps, 5)
            dve.memset(kb[:, 0].bitcast(F32), 0.0)
            steps = Steps(dve, q_steps, 0)
            square_sums_q(0, 0)
            steps.then(square_sums_q(0, 1))
            heads_ = slice(0, QH)
            guess(steps, heads_)
            refine(steps, heads_)
            newton(steps, heads_)
            assert steps.n == Q_STEPS
            queries(0)
            stack_keys(0)
            q_low(0)
            norm1_statistics(1, 1, 1)
            maxima(0, 0, UNITS - 1)
            split_maxima(0)
            rounds(dve, one_round)
            last = BLOCKS - 1
            ot_low(last)
            for hf in range(2):
                residual(last, 1, hf)
            norm2_statistics(last)
            dve.wait_ge(rs2_ready, BLOCKS)
            for j in range(J // 2, J):
                ins = dve.tensor_scalar(xn[:, j, :], x2[:, j, :], rs[:, 1, j:j + 1], nb[:, 1, j:j + 1],
                                        ALU.mult, ALU.add)
            ins.then_inc(xn2_half_ready, 1)
            mix(last, 1, xk, xk_begun, xk_ready, AUX_MU_K)
            mix(last, 1, xr, xr_begun, xr_ready, AUX_MU_R)
            dve.wait_ge(kact_copied, BLOCKS)
            dve.tensor_tensor(qh[:, :, :], xd[:, :, :], ot[:, :, :].bitcast(F32), ALU.subtract).then_inc(kact_split, 1)
            for hf in range(2):
                gate_values(last, hf)
                dve.wait_ge(gated, 2 * last + hf + 3)
                dve.tensor_tensor(half_of(rt, hf), half_of(rt, hf), half_of(x2, hf), ALU.add).then_inc(last_ready, 1)

        @block.gpsimd
        def _(pool):
            def rstd(which, t, ready, done, steps_sem):
                pool.wait_ge(ready, t + 1)
                steps = Steps(pool, steps_sem, 2 * t)
                pool.tensor_tensor(nm[:, which, :], mv[:, which, :, 0], minus_one[:, :], ALU.mult)
                steps.then(pool.tensor_tensor(ve[:, which, :], mv[:, which, :, 1], eps[:, :], ALU.add))
                steps.then(pool.tensor_tensor(rs[:, which, :], ve[:, which, :], minus_half[:, :], ALU.pow))
                pool.tensor_tensor(nb[:, which, :], nm[:, which, :], rs[:, which, :], ALU.mult).then_inc(done, 1)

            def with_bias(t, par, loads):
                wait(pool, x2_ready, 2 * (t - 1))
                pool.wait_ge(x_landed[par], 16 * loads)
                pool.tensor_tensor(xb[:, par], x_in[:, par],
                                   aux_sb[:, AUX_BP:AUX_BP + C].unsqueeze(1).broadcast_to([P, J, C]),
                                   ALU.add).then_inc(xb_ready, 1)

            def scale_keys(b, deviations_ready, count):
                steps = Steps(pool, pk_steps, KP_STEPS * b)
                kh, kth = (t_[:, :, :].rearrange("p a (h d) -> p (a h) d", d=D) for t_ in (kf, kt))
                g, bb = (aux_sb[:, a:a + D].unsqueeze(1).broadcast_to([P, 2 * H, D]) for a in (AUX_G, AUX_B))
                gsc, bsc = (gs[:, n, :].unsqueeze(1).broadcast_to([P, 2 * H, D]) for n in range(2))
                deviations = qst[:, 2, QH:QH + KH].unsqueeze(2).broadcast_to([P, KH, D])
                pool.wait_ge(deviations_ready, count)
                steps.then(pool.tensor_tensor(kh, kh, deviations, ALU.mult))
                steps.then(pool.tensor_tensor(kh, kh, g, ALU.mult))
                steps.then(pool.tensor_tensor(kh, kh, bb, ALU.add))
                pool.tensor_tensor(kth, kh, bsc, ALU.mult).then_inc(k_products, 1)
                pool.wait_ge(k_products, b + 1)
                pool.tensor_tensor(kh, kh, gsc, ALU.mult).then_inc(k_scaled, 1)

            def kact_low(t, last_stack):
                pool.wait_ge(kact_copied, t + 1)
                pool.wait_ge(stacked, 16 * 12 * (last_stack + 1))
                pool.tensor_tensor(qh[:, :, :], xd[:, :, :], ot[:, :, :].bitcast(F32), ALU.subtract).then_inc(kact_split, 1)

            def output(t):
                for hf in range(2):
                    pool.wait_ge(gated, 2 * t + hf + 3)
                    half = slice(2 * hf, 2 * hf + 2)
                    pool.tensor_tensor(rt[:, half], rt[:, half], x2[:, half], ALU.add).then_inc(out_ready, 1)
                pool.wait_ge(out_ready, 2 * (t + 1) + 1)
                pool.dma_start(out_rows[t], rt[:, :, :]).then_inc(stored, 16)

            def one_round(t, b, par, finish, prepare):
                if finish:
                    rstd(1, t - 1, mv2_ready, rs2_ready, p2_steps)
                if prepare and par == 1:
                    scale_keys(b, q_steps, Q_STEPS * (t + 2))
                if prepare:
                    with_bias(t + 1, 1 - par, b + 1)
                if finish:
                    kact_low(t - 1, t + 1 if prepare else t)
                if prepare:
                    rstd(0, t + 2, mv1_ready, rs1_ready, p1_steps)
                if finish:
                    output(t - 1)

            steps = Steps(pool, zeroed, 0)
            steps.then(pool.memset(cx[:, :, M:2 * P], 0.0))
            steps.then(pool.memset(eps[:, :], EPS))
            steps.then(pool.memset(minus_half[:, :], -0.5))
            steps.then(pool.memset(minus_one[:, :], -1.0))
            steps.then(pool.memset(vm[:, 0], 0.0))
            rstd(0, 0, mv1_ready, rs1_ready, p1_steps)
            steps.then(pool.memset(vm[:, 0, :, D:D + 1], 1.0))
            steps.then(pool.memset(vr[:, 0], 0.0))
            for k in range(4):
                steps.then(pool.memset(vr[SLOT * k:SLOT * k + M1, 0, :, SLOT * k + D:SLOT * k + D + 1], 1.0))
            steps.then(pool.memset(kr[:, 0].bitcast(F32), 0.0))
            steps.then(pool.memset(x2t[:, 0, :, 0:1], 0.0))
            steps.then(pool.memset(xq[ROW_ONE:ROW_MAX, 1].bitcast(F32), 1.0))
            assert steps.n == ZEROED
            pool.memset(spare2[:, :], 0.0).then_inc(out_ready, 1)
            pool.wait_ge(out_ready, 1)
            pool.dma_start(spare2[:, :], aux[:, 0:2]).then_inc(stored, 16)
            pool.wait_ge(w_steps, 3)
            scale_keys(0, k0_steps, Q_STEPS)
            with_bias(0, 0, 1)
            for n, (high, low, weight) in enumerate(((wp_high, wp_low, WP), (wv_high, wv_low, FV))):
                pool.wait_ge(w_high, n + 1)
                pool.tensor_tensor(low[:, :, :], w[:, :, weight, :], high[:, :, :].bitcast(F32),
                                   ALU.subtract).then_inc(w_split, 1)
            rstd(0, 1, mv1_ready, rs1_ready, p1_steps)
            rounds(pool, one_round)
            rstd(1, BLOCKS - 1, mv2_ready, rs2_ready, p2_steps)


def kernel(x, ctx_1024, L0_xattn_Wq, L0_xattn_Wk, L0_xattn_Wv, L0_xattn_Wp, L0_xattn_bp, L0_xattn_ln_g,
           L0_xattn_ln_b, L0_ffn_W_r, L0_ffn_W_k, L0_ffn_W_v, L0_ffn_mu_r, L0_ffn_mu_k):
    import concourse.bacc as bacc
    from concourse.bass_utils import run_bass_kernel_spmd

    def spread(row):
        return np.broadcast_to(np.asarray(row)[None, :], (P, row.shape[0]))

    def column(vector):
        return np.asarray(vector).reshape(KC, P).T

    stacked = np.stack([np.asarray(m).T for m in (L0_xattn_Wq, L0_xattn_Wk, L0_xattn_Wv, L0_xattn_Wp,
                                                  L0_ffn_W_r, L0_ffn_W_k, L0_ffn_W_v)])
    arrays = {
        "x": np.concatenate([np.asarray(x).reshape(B * N, C), np.zeros((T, C), np.float32)]),
        "context": np.ascontiguousarray(np.asarray(ctx_1024).reshape(B, M, KC, P).transpose(0, 3, 2, 1)),
        "weights": np.ascontiguousarray(stacked.reshape(NW, KC, P, C).transpose(2, 1, 0, 3)),
        "aux": np.ascontiguousarray(np.concatenate(
            [column(L0_ffn_mu_r), column(L0_ffn_mu_k), spread(L0_xattn_ln_g), spread(L0_xattn_ln_b),
             spread(L0_xattn_bp), np.eye(P, dtype=np.float32)], axis=1)),
    }
    nc = bacc.Bacc("TRN2", target_bir_lowering=False, num_devices=1)
    args = [nc.dram_tensor(name, a.shape, mybir.dt.from_np(a.dtype), kind="ExternalInput").ap()
            for name, a in arrays.items()]
    out = nc.dram_tensor("out", (B * N, C), F32, kind="ExternalOutput").ap()
    xattn_ffn(nc, *args, out)
    result = run_bass_kernel_spmd(nc, [arrays], core_ids=[0])
    return result.results[0]["out"].reshape(B, N, C)
```
